# Optimizing a Trainium2 kernel written in Bass

```python
import numpy as np
import jax
import jax.numpy as jnp

def _softmax(x, axis=-1):
    return jax.nn.softmax(x, axis=axis)

def _gelu(x):
    return jax.nn.gelu(x, approximate=True)

def _silu(x):
    return jax.nn.silu(x)

def _sigmoid(x):
    return jax.nn.sigmoid(x)

def _layernorm(x, axis=-1, eps=1e-05):
    m = jnp.mean(x, axis=axis, keepdims=True)
    v = jnp.var(x, axis=axis, keepdims=True)
    return (x - m) / jnp.sqrt(v + eps)

def _scatter_add(tgt, idx, src, axis=0):
    return tgt.at[idx].add(src)

def _segment_sum(src, seg, n):
    return jax.ops.segment_sum(src, seg, n)
kernel_name = 'mk_recurrent_d1_jaxref_r4_4f911b'

def setup_inputs(seed: int=0):
    np.random.seed(seed)
    _w = jnp.asarray

    def _L0_attn_setup():
        import jax, jax.numpy as jnp
        import numpy as np
        D_MODEL = 512
        N_HEADS = 16
        D_HEAD = D_MODEL // N_HEADS
        B, S = (2, 512)
        EPS = 1e-05

        def _mhsa(X, ln_g, ln_b, Wq, bq, Wk, bk, Wv, bv, Wo, bo):
            n_ctx = X.shape[-2]
            mu = jnp.mean(X, axis=-1, keepdims=True)
            var = jnp.mean(jnp.square(X - mu), axis=-1, keepdims=True)
            Xn = (X - mu) * jax.lax.rsqrt(var + EPS) * ln_g + ln_b

            def split_heads(t):
                return t.reshape(t.shape[:-1] + (N_HEADS, D_HEAD)).swapaxes(-2, -3)
            Q = split_heads(Xn @ Wq + bq)
            K = split_heads(Xn @ Wk + bk)
            V = split_heads(Xn @ Wv + bv)
            scores = jnp.einsum('bhqd,bhkd->bhqk', Q, K) / jnp.sqrt(jnp.float32(D_HEAD))
            causal = jnp.tril(jnp.ones((n_ctx, n_ctx), dtype=bool))
            scores = jnp.where(causal, scores, jnp.float32(-jnp.inf))
            A = jax.nn.softmax(scores, axis=-1)
            AV = jnp.einsum('bhqk,bhkd->bhqd', A, V)
            AV = AV.swapaxes(-2, -3).reshape(X.shape[:-1] + (D_MODEL,))
            return AV @ Wo + bo
        key = jax.random.key(seed)
        ks = jax.random.split(key, 10)
        sd = 1.0 / np.sqrt(D_MODEL)
        inp = {'X': jax.random.normal(ks[0], (B, S, D_MODEL), dtype=jnp.float32), 'ln_g': jnp.ones((D_MODEL,), jnp.float32), 'ln_b': jnp.zeros((D_MODEL,), jnp.float32), 'Wq': jax.random.uniform(ks[1], (D_MODEL, D_MODEL), jnp.float32, -sd, sd), 'bq': jax.random.uniform(ks[2], (D_MODEL,), jnp.float32, -sd, sd), 'Wk': jax.random.uniform(ks[3], (D_MODEL, D_MODEL), jnp.float32, -sd, sd), 'bk': jax.random.uniform(ks[4], (D_MODEL,), jnp.float32, -sd, sd), 'Wv': jax.random.uniform(ks[5], (D_MODEL, D_MODEL), jnp.float32, -sd, sd), 'bv': jax.random.uniform(ks[6], (D_MODEL,), jnp.float32, -sd, sd), 'Wo': jax.random.uniform(ks[7], (D_MODEL, D_MODEL), jnp.float32, -sd, sd), 'bo': jax.random.uniform(ks[8], (D_MODEL,), jnp.float32, -sd, sd)}
        return inp
    _L0_attn_in = _L0_attn_setup()

    def _L0_ffn_setup():
        import jax, jax.numpy as jnp
        import numpy as np
        B, S, D, H = (8, 1024, 512, 1280)

        def ternarize_weight(w):
            abs_mean = jnp.maximum(jnp.mean(jnp.abs(w)), 1e-05)
            thr = 0.7 * abs_mean
            one = jnp.ones((), dtype=w.dtype)
            q = jnp.where(w > thr, one, jnp.where(w < -thr, -one, jnp.zeros((), dtype=w.dtype)))
            return w + jax.lax.stop_gradient(q * abs_mean - w)
        key = jax.random.key(seed)
        k1, k2, k3 = jax.random.split(key, 3)
        x = jax.random.normal(k1, (B, S, D), dtype=jnp.float32)
        w_fc = jax.random.normal(k2, (H, D), dtype=jnp.float32) / np.sqrt(D).astype(np.float32)
        w_proj = jax.random.normal(k3, (D, H), dtype=jnp.float32) / np.sqrt(H).astype(np.float32)
        return {'x': x, 'w_fc': w_fc, 'w_proj': w_proj}
    _L0_ffn_in = _L0_ffn_setup()
    _d = {'L0_attn_X': _L0_attn_in['X'], 'L0_attn_ln_g': _L0_attn_in['ln_g'], 'L0_attn_ln_b': _L0_attn_in['ln_b'], 'L0_attn_Wq': _L0_attn_in['Wq'], 'L0_attn_bq': _L0_attn_in['bq'], 'L0_attn_Wk': _L0_attn_in['Wk'], 'L0_attn_bk': _L0_attn_in['bk'], 'L0_attn_Wv': _L0_attn_in['Wv'], 'L0_attn_bv': _L0_attn_in['bv'], 'L0_attn_Wo': _L0_attn_in['Wo'], 'L0_attn_bo': _L0_attn_in['bo'], 'L0_ffn_w_fc': _L0_ffn_in['w_fc'], 'L0_ffn_w_proj': _L0_ffn_in['w_proj']}
    _x0 = _d['L0_attn_X']
    _d['L0_attn_X'] = jax.random.normal(jax.random.fold_in(jax.random.key(seed), 1), (2, 2048, 512), dtype=_x0.dtype)
    del _x0
    return _d

def reference(L0_attn_X, L0_attn_ln_g, L0_attn_ln_b, L0_attn_Wq, L0_attn_bq, L0_attn_Wk, L0_attn_bk, L0_attn_Wv, L0_attn_bv, L0_attn_Wo, L0_attn_bo, L0_ffn_w_fc, L0_ffn_w_proj):

    def _L0_attn_ref(X, ln_g, ln_b, Wq, bq, Wk, bk, Wv, bv, Wo, bo):
        import jax, jax.numpy as jnp
        import numpy as np
        D_MODEL = 512
        N_HEADS = 16
        D_HEAD = D_MODEL // N_HEADS
        B, S = (2, 512)
        EPS = 1e-05

        def _mhsa(X, ln_g, ln_b, Wq, bq, Wk, bk, Wv, bv, Wo, bo):
            n_ctx = X.shape[-2]
            mu = jnp.mean(X, axis=-1, keepdims=True)
            var = jnp.mean(jnp.square(X - mu), axis=-1, keepdims=True)
            Xn = (X - mu) * jax.lax.rsqrt(var + EPS) * ln_g + ln_b

            def split_heads(t):
                return t.reshape(t.shape[:-1] + (N_HEADS, D_HEAD)).swapaxes(-2, -3)
            Q = split_heads(Xn @ Wq + bq)
            K = split_heads(Xn @ Wk + bk)
            V = split_heads(Xn @ Wv + bv)
            scores = jnp.einsum('bhqd,bhkd->bhqk', Q, K) / jnp.sqrt(jnp.float32(D_HEAD))
            causal = jnp.tril(jnp.ones((n_ctx, n_ctx), dtype=bool))
            scores = jnp.where(causal, scores, jnp.float32(-jnp.inf))
            A = jax.nn.softmax(scores, axis=-1)
            AV = jnp.einsum('bhqk,bhkd->bhqd', A, V)
            AV = AV.swapaxes(-2, -3).reshape(X.shape[:-1] + (D_MODEL,))
            return AV @ Wo + bo
        return _mhsa(X, ln_g, ln_b, Wq, bq, Wk, bk, Wv, bv, Wo, bo)

    def _L0_ffn_ref(x, w_fc, w_proj):
        import jax, jax.numpy as jnp
        import numpy as np
        B, S, D, H = (8, 1024, 512, 1280)

        def ternarize_weight(w):
            abs_mean = jnp.maximum(jnp.mean(jnp.abs(w)), 1e-05)
            thr = 0.7 * abs_mean
            one = jnp.ones((), dtype=w.dtype)
            q = jnp.where(w > thr, one, jnp.where(w < -thr, -one, jnp.zeros((), dtype=w.dtype)))
            return w + jax.lax.stop_gradient(q * abs_mean - w)
        h = jnp.einsum('bsd,hd->bsh', x, ternarize_weight(w_fc))
        h = jnp.square(jax.nn.relu(h))
        return jnp.einsum('bsh,dh->bsd', h, ternarize_weight(w_proj))
    x = L0_attn_X
    xn = _layernorm(x, axis=-1)
    s = _L0_attn_ref(xn, L0_attn_ln_g, L0_attn_ln_b, L0_attn_Wq, L0_attn_bq, L0_attn_Wk, L0_attn_bk, L0_attn_Wv, L0_attn_bv, L0_attn_Wo, L0_attn_bo)
    g = _silu(_L0_ffn_ref(xn, L0_ffn_w_fc, L0_ffn_w_proj))
    x = x + s * g
    return x

_drawn_inputs = setup_inputs


def setup_inputs(seed=0):
    import zlib

    import numpy as np

    out = dict(_drawn_inputs(seed))
    spreads = {'L0_attn_ln_g': (1.0, 0.6), 'L0_attn_ln_b': (0.0, 0.1)}
    factors = {'L0_attn_Wq': 5.392,
     'L0_attn_bq': 8.0,
     'L0_attn_Wk': 5.366,
     'L0_attn_bk': 8.0,
     'L0_attn_bv': 3.82}
    for name, (base, spread) in spreads.items():
        noise = np.random.default_rng([zlib.crc32(name.encode()), seed]).standard_normal(out[name].shape)
        drawn = base * np.exp(spread * noise) if base else spread * noise
        out[name] = jnp.asarray(drawn.astype(out[name].dtype))
    for name, factor in factors.items():
        out[name] = (out[name] * factor).astype(out[name].dtype)
    return out
```

```python
from contextlib import ExitStack

import numpy as np

import concourse.bass as bass
from concourse import mybir
from concourse.alu_op_type import AluOpType as ALU

ACT = mybir.ActivationFunctionType
F32 = mybir.dt.float32
F16 = mybir.dt.float16
BF16 = mybir.dt.bfloat16
I32 = mybir.dt.int32
AX = mybir.AxisListType

P = 128
B, S, D = 2, 2048, 512
H, DH = 16, 32
HID = 1280
KT = D // P
HT = HID // P
NT = B * S // P
G = 512
JT = G // P
CH = S // G
UNITS = B * H
EPS = 1e-5
BIG = 1e30
VW = 2 * DH + 1
V_SHIFT = 2.0 ** -9
RMAX = bass.bass_isa.ReduceOp.max
Q, K, V, O = range(4)


class Steps:

    def __init__(self, eng, sem, base=0):
        self.eng, self.sem, self.base, self.n = eng, sem, base, 0

    def did(self, instruction):
        instruction.then_inc(self.sem, 1)
        self.n += 1

    def settle(self):
        self.eng.wait_ge(self.sem, self.base + self.n)


def bare(eng, sem):
    eng.sem_inc(sem)


def weights_block(nc, ins, kept):
    (ln_g, ln_b, wq, bq, wk, bk, wv, bv, wo, bo, w_fc, w_proj) = ins
    with ExitStack() as ctx:
        def sb(name, shape, dt):
            return ctx.enter_context(nc.sbuf_tensor(name, shape, dt))

        def sem(name):
            return ctx.enter_context(nc.semaphore(name))

        wf = sb("w_raw", [P, 4, KT, D], F32)
        wg = sb("w_gained", [P, 3, KT, D], F32)
        fc = sb("w_fc_raw", [P, HT, D], F32)
        pr = sb("w_proj_raw", [P, KT, HID], F32)
        fc_neg = sb("fc_neg", [P, HT, D], F16)
        pr_neg = sb("pr_neg", [P, KT, HID], F16)
        fc_t = sb("fc_ternary", [P, HT, D], F16)
        pr_t = sb("pr_ternary", [P, KT, HID], F16)
        vecs = sb("vectors", [P, 5, KT], F32)
        bo_row = sb("bo_row", [P, D], F32)
        amax = sb("amax", [P, 4], F32)
        gmax = sb("gmax", [P, 4], F32)
        pw = sb("pw", [P, 4], F32)
        rpw = sb("rpw", [P, 4], F32)
        asum = sb("asum", [P, 2], F32)
        thr = sb("thr", [P, 2], F32)
        nthr = sb("nthr", [P, 2], F32)
        am2 = sb("am2", [P, 2], F32)
        ones = sb("ones", [P, P], F32)
        vb = sb("v_bias", [P, KT], F32)
        vb_wide = sb("v_bias_wide", [P, KT, P], F32)

        tp = ctx.enter_context(nc.psum_tensor("w_tp", [P, 4, 2, 512], F16))
        pb = ctx.enter_context(nc.psum_tensor("w_bias", [P, 512], F32))
        ps = ctx.enter_context(nc.psum_tensor("w_sum", [P, 512], F32))
        po = ctx.enter_context(nc.psum_tensor("w_obias", [P, 512], F32))

        ld_w = [sem(f"ld_w{m}") for m in range(4)]
        ld_vec = sem("ld_vec")
        ld_fc, ld_pr, ld_bo = sem("ld_fc"), sem("ld_pr"), sem("ld_bo")
        s_pool = sem("s_pool")
        s_ones = sem("s_ones")
        s_gain = sem("s_gain")
        s_amax = sem("s_amax")
        s_gmax = sem("s_gmax")
        s_scale = sem("s_scale")
        s_head = sem("s_head")
        s_asum = sem("s_asum")
        s_sum = sem("s_sum")
        s_thr = sem("s_thr")
        s_tern = sem("s_tern")
        s_tp, s_tc = sem("s_tp"), sem("s_tc")
        s_bias = sem("s_bias")
        s_vbw = sem("s_vbw")
        s_obias = sem("s_obias")
        s_dve = sem("s_dve")

        with nc.Block() as block:
            @block.sync
            def _(sp):
                for m, w in enumerate((wq, wk, wv)):
                    sp.dma_start(wf[:, m], w.rearrange("(k p) n -> p k n", p=P)).then_inc(ld_w[m], 16)
                with nc.allow_non_contiguous_dma(reason="five short vectors as columns"):
                    for n, v in enumerate((ln_g, ln_b, bq, bk, bv)):
                        sp.dma_start(vecs[:, n], v.rearrange("(k p) -> p k", p=P)).then_inc(ld_vec, 16)
                sp.dma_start(fc[:], w_fc.rearrange("(k p) n -> p k n", p=P)).then_inc(ld_fc, 16)
                sp.dma_start(pr[:], w_proj.rearrange("(k p) n -> p k n", p=P)).then_inc(ld_pr, 16)
                sp.dma_start(wf[:, O], wo.rearrange("(k p) n -> p k n", p=P)).then_inc(ld_w[O], 16)
                sp.dma_start(bo_row[:], bo.rearrange("(a n) -> a n", a=1).to_broadcast([P, D])).then_inc(ld_bo, 16)

            @block.gpsimd
            def _(pool):
                own = Steps(pool, s_pool)
                own.did(nc.gpsimd.memset(ones[:], 1.0))
                for t in (kept["ident32"], kept["ident16"], kept["identb"], kept["mask_kq"], kept["mask_qk"]):
                    own.did(nc.gpsimd.memset(t[:], 0.0))
                own.did(nc.gpsimd.memset(kept["half"][:], -0.5))
                own.settle()
                for t in (kept["ident32"], kept["ident16"], kept["identb"]):
                    nc.gpsimd.affine_select(out=t[:], in_=t[:], compare_op=ALU.not_equal, fill=1.0, base=0,
                                            pattern=[[-1, P]], channel_multiplier=1).then_inc(s_ones, 1)
                nc.gpsimd.affine_select(out=kept["mask_kq"][:], in_=kept["mask_kq"][:], compare_op=ALU.is_ge, fill=-BIG,
                                        base=0, pattern=[[1, P]], channel_multiplier=-1).then_inc(s_ones, 1)
                nc.gpsimd.affine_select(out=kept["mask_qk"][:], in_=kept["mask_qk"][:], compare_op=ALU.is_ge, fill=-BIG,
                                        base=0, pattern=[[-1, P]], channel_multiplier=1).then_inc(s_ones, 1)
                for m in range(4):
                    pool.wait_ge(s_amax, m + 1)
                    nc.gpsimd.partition_all_reduce(gmax[:, m:m + 1], amax[:, m:m + 1], P, RMAX).then_inc(s_gmax, 1)

            @block.scalar
            def _(act):
                def head(m):
                    act.wait_ge(s_scale, m + 1)
                    src = wg[:, m] if m < 3 else wf[:, O]
                    nc.scalar.activation(kept["w_head"][:, m] if m < 3 else kept["wo_head"][:], src, ACT.Identity,
                                         scale=kept["scale"][:, m:m + 1]).then_inc(s_head, 1)

                for m in range(3):
                    head(m)
                for n in range(20):
                    act.wait_ge(s_tp, n + 1)
                    if n < 10:
                        dst = kept["fc_T"][:, :, n * P:(n + 1) * P]
                    else:
                        dst = kept["proj_T"][:, n - 10, :].rearrange("p (k n) -> p k n", k=KT)
                    nc.scalar.activation(dst, tp[:, n % 4, 0].rearrange("p (k n) -> p k n", k=4), ACT.Copy).then_inc(s_tc, 1)
                head(O)

            @block.vector
            def _(dve):
                own = Steps(dve, s_dve)

                def scales(m):
                    dve.wait_ge(s_gmax, m + 1)
                    c = slice(m, m + 1)
                    own.did(nc.vector.tensor_scalar(gmax[:, c], gmax[:, c], 1e-30, None, ALU.max))
                    own.settle()
                    own.did(nc.vector.tensor_single_scalar(pw[:, c].bitcast(I32), gmax[:, c].bitcast(I32), 0x7F800000, ALU.bitwise_and))
                    own.settle()
                    own.did(nc.vector.reciprocal(rpw[:, c], pw[:, c]))
                    own.settle()
                    own.did(nc.vector.tensor_scalar(kept["scale"][:, c], rpw[:, c], 2.0 ** 14, None, ALU.mult))
                    own.settle()
                    nc.vector.tensor_scalar(kept["unscale"][:, c], pw[:, c], 2.0 ** -14, None, ALU.mult).then_inc(s_scale, 1)

                def tail(m):
                    dve.wait_ge(s_head, m + 1)
                    src = wg[:, m] if m < 3 else wf[:, O]
                    hi, lo = (kept["w_head"][:, m], kept["w_tail"][:, m]) if m < 3 else (kept["wo_head"][:], kept["wo_tail"][:])
                    own.did(nc.vector.scalar_tensor_tensor(lo, src, kept["scale"][:, m:m + 1], hi, ALU.mult, ALU.subtract))

                dve.wait_ge(ld_vec, 80)
                for m in range(3):
                    dve.wait_ge(ld_w[m], 16)
                    for k in range(KT):
                        own.did(nc.vector.tensor_scalar(wg[:, m, k], wf[:, m, k], vecs[:, 0, k:k + 1], None, ALU.mult))
                    own.settle()
                    nc.vector.tensor_reduce(amax[:, m:m + 1], wg[:, m], AX.XY, ALU.max, apply_absolute_value=True).then_inc(s_amax, 1)
                    if m:
                        scales(m - 1)
                        if m > 1:
                            tail(m - 2)
                scales(2)
                tail(1)
                dve.wait_ge(ld_fc, 16)
                nc.vector.tensor_reduce(asum[:, 0:1], fc[:], AX.XY, ALU.add, apply_absolute_value=True).then_inc(s_asum, 1)
                dve.wait_ge(ld_pr, 16)
                nc.vector.tensor_reduce(asum[:, 1:2], pr[:], AX.XY, ALU.add, apply_absolute_value=True).then_inc(s_asum, 1)
                tail(2)
                dve.wait_ge(s_sum, 1)
                own.did(nc.vector.tensor_scalar(kept["amean"][:], ps[:, 0:2], 1.0 / (HID * D), 1e-5, ALU.mult, ALU.max))
                own.settle()
                own.did(nc.vector.tensor_scalar(thr[:], kept["amean"][:], 0.7, None, ALU.mult))
                own.settle()
                own.did(nc.vector.tensor_scalar(nthr[:], thr[:], -1.0, None, ALU.mult))
                own.settle()
                for raw, neg, out, c in ((fc, fc_neg, fc_t, 0), (pr, pr_neg, pr_t, 1)):
                    own.did(nc.vector.tensor_scalar(neg[:], raw[:], nthr[:, c:c + 1], None, ALU.is_lt))
                    own.settle()
                    nc.vector.scalar_tensor_tensor(out[:], raw[:], thr[:, c:c + 1], neg[:], ALU.is_gt, ALU.subtract).then_inc(s_tern, 1)
                dve.wait_ge(s_bias, 1)
                bc = pb[:, 0:12].rearrange("p (m k) -> p m k", m=3)
                nc.vector.tensor_tensor(kept["qk_bias"][:], bc[:, 0:2], vecs[:, 2:4], ALU.add).then_inc(s_dve, 1)
                own.n += 1
                own.did(nc.vector.tensor_tensor(vb[:], bc[:, 2], vecs[:, 4], ALU.add))
                own.settle()
                nc.vector.tensor_copy(vb_wide[:], vb[:].rearrange("p (k a) -> p k a", a=1).to_broadcast([P, KT, P])).then_inc(s_vbw, 1)
                dve.wait_ge(ld_w[O], 16)
                nc.vector.tensor_reduce(amax[:, O:O + 1], wf[:, O], AX.XY, ALU.max, apply_absolute_value=True).then_inc(s_amax, 1)
                scales(O)
                tail(O)
                own.did(nc.vector.tensor_tensor(am2[:, 0:1], kept["amean"][:, 0:1], kept["amean"][:, 0:1], ALU.mult))
                own.settle()
                own.did(nc.vector.tensor_tensor(am2[:, 1:2], am2[:, 0:1], kept["amean"][:, 1:2], ALU.mult))
                own.settle()
                own.did(nc.vector.tensor_scalar(kept["ffn_scale"][:], am2[:, 1:2], 8.0, None, ALU.mult))
                own.did(nc.vector.scalar_tensor_tensor(kept["out_scale"][:], kept["unscale"][:, V:V + 1], 1.0 / V_SHIFT,
                                                       kept["unscale"][:, O:O + 1], ALU.mult, ALU.mult))
                dve.wait_ge(s_obias, 1)
                dve.wait_ge(ld_bo, 16)
                own.did(nc.vector.tensor_tensor(kept["out_bias"][:], po[:], bo_row[:], ALU.add))

            @block.tensor
            def _(pe):
                pe.wait_ge(ld_vec, 80)
                for m in range(3):
                    pe.wait_ge(ld_w[m], 16)
                    for mt in range(KT):
                        for k in range(KT):
                            last = nc.tensor.matmul(pb[:, 4 * m + mt:4 * m + mt + 1], wf[:, m, k, mt * P:(mt + 1) * P],
                                                    vecs[:, 1, k:k + 1], start=(k == 0), stop=(k == KT - 1))
                last.then_inc(s_bias, 1)
                pe.wait_ge(s_asum, 2)
                pe.wait_ge(s_pool, 7)
                nc.tensor.matmul(ps[:, 0:2], ones[:], asum[:], start=True, stop=True).then_inc(s_sum, 1)
                pe.wait_ge(s_ones, 5)
                for n in range(20):
                    if n % 10 == 0:
                        pe.wait_ge(s_tern, n // 10 + 1)
                    if n >= 4:
                        pe.wait_ge(s_tc, n - 3)
                    for k in range(4):
                        src = fc_t[:, n, k * P:(k + 1) * P] if n < 10 else pr_t[:, k, (n - 10) * P:(n - 9) * P]
                        last = nc.tensor.transpose(tp[:, n % 4, 0, k * P:(k + 1) * P], src, kept["ident16"][:])
                    last.then_inc(s_tp, 1)
                pe.wait_ge(s_vbw, 1)
                pe.wait_ge(ld_w[O], 16)
                for k in range(KT):
                    last = nc.tensor.matmul(po[:], vb_wide[:, k], wf[:, O, k], start=(k == 0), stop=(k == KT - 1))
                last.then_inc(s_obias, 1)


T_PER, PJ_PER, QK_PER = 2 * JT, 3 * KT, 2 * KT
RING = 4
GROUPS = B * CH


def project_block(nc, x, qk_dram, xf_dram, kept):
    with ExitStack() as ctx:
        def sb(name, shape, dt):
            return ctx.enter_context(nc.sbuf_tensor(name, shape, dt))

        def sem(name):
            return ctx.enter_context(nc.semaphore(name))

        xin = sb("xin", [P, 2, JT, D], F32)
        xn = sb("xn", [P, JT, D], F32)
        xn2 = sb("xn2", [P, JT, D], F32)
        st6 = sb("st6", [P, JT, 6], F32)
        mv = sb("mv", [P, JT, 2], F32)
        va = sb("va", [P, JT], F32)
        r1 = sb("r1", [P, JT], F32)
        vb = sb("vb", [P, JT], F32)
        vc = sb("vc", [P, JT], F32)
        vd = sb("vd", [P, JT], F32)
        r2 = sb("r2", [P, JT], F32)
        f_head = sb("f_head", [P, 2, KT, G], F16)
        f_tail = sb("f_tail", [P, 2, KT, G], F16)
        a_head = sb("a_head", [P, 2, KT, G], F16)
        a_tail = sb("a_tail", [P, 2, KT, G], F16)
        qk32 = sb("qk32", [P, RING, G], F32)
        qk_head = sb("qk_head", [P, RING, G], F16)
        qk_tail = sb("qk_tail", [P, RING, G], F16)
        tps = ctx.enter_context(nc.psum_tensor("tps", [P, RING, 512], F32))
        pjs = ctx.enter_context(nc.psum_tensor("pjs", [P, RING, 512], F32))
        v_all = kept["v_all"]

        ld_x = [sem(f"ld_x{u}") for u in range(2)]
        s_va, s_r1, s_vd, s_r2 = sem("s_va"), sem("s_r1"), sem("s_vd"), sem("s_r2")
        s_xn, s_xn2 = sem("s_xn"), sem("s_xn2")
        s_ones = sem("s_v_ones")
        s_bare = sem("s_bare")
        s_own = sem("s_own")
        s_t = sem("s_t")
        s_th, s_tt = sem("s_th"), sem("s_tt")
        s_pj = sem("s_pj")
        s_pa = sem("s_pa")
        s_ph = sem("s_ph")
        s_pt = sem("s_pt")
        st_qk = [sem(f"st_qk{r}") for r in range(RING)]
        st_xf = [sem(f"st_xf{u}") for u in range(2)]

        OWN_PER = 2 * JT + 2

        def groups(eng, body):
            with eng.Fori(0, CH - 1) as it:
                for u in range(2):
                    body(it * 2 + u, it, u, True)
            for u in range(2):
                body(GROUPS - 2 + u, CH - 1, u, u == 0)

        def nxt(it, u):
            return (it, 1) if u == 0 else (it + 1, 0)

        with nc.Block() as block:
            @block.sync
            def _(sp):
                for r in range(RING):
                    sp.sem_inc(st_qk[r], 32)
                for u in range(2):
                    sp.sem_inc(st_xf[u], 64)

                def load_x(it, u):
                    sp.dma_start(xin[:, u], x[u, bass.ds(it * G, G), :].rearrange("(j p) d -> p j d", p=P)).then_inc(ld_x[u], 16)

                def store_xf(it, u):
                    for h in range(2):
                        for part, src in enumerate((f_head, f_tail)):
                            sp.dma_start(xf_dram[bass.ds(it * 2 + (8 * u + h), 1), :, part],
                                         src[:, u, :, 256 * h:256 * (h + 1)]).then_inc(st_xf[u], 16)

                load_x(0, 0)
                load_x(0, 1)
                sp.wait_ge(s_tt, T_PER)
                store_xf(0, 0)

                def body(g, it, u, more):
                    if more and not (isinstance(it, int) and it == CH - 1):
                        sp.wait_ge(s_xn, g * JT + JT)
                        load_x(it + 1, u)
                    for i in range(QK_PER):
                        sp.wait_ge(s_pt, g * PJ_PER + (RING + i + 1))
                        for part, src in enumerate((qk_head, qk_tail)):
                            first = 16 * u + 4 * (i % KT)
                            sp.dma_start(qk_dram[first:first + 4, i // KT, part, :, bass.ds(it * G, G)],
                                         src[:, i % RING]).then_inc(st_qk[i % RING], 16)
                    if more:
                        sp.wait_ge(s_tt, g * T_PER + 2 * T_PER)
                        store_xf(*nxt(it, u))
                groups(sp, body)
                for r in range(RING):
                    sp.wait_ge(st_qk[r], 32 + 32 * GROUPS * QK_PER // RING)
                for u in range(2):
                    sp.wait_ge(st_xf[u], 64 + 64 * CH)

            @block.gpsimd
            def _(pool):
                def norms(g):
                    pool.wait_ge(s_va, g + 1)
                    nc.gpsimd.tensor_tensor(r1[:], va[:], kept["half"][:], ALU.pow).then_inc(s_r1, 1)
                    pool.wait_ge(s_vd, g + 1)
                    nc.gpsimd.tensor_tensor(r2[:], vd[:], kept["half"][:], ALU.pow).then_inc(s_r2, 1)

                def second(g, first):
                    pool.wait_ge(s_r2, g + 1)
                    for j in range(JT):
                        pool.wait_ge(s_xn, g * JT + (j + 1))
                        if not first:
                            pool.wait_ge(s_t, g * T_PER + (2 * j + 2 - T_PER))
                        bare(pool, s_bare)
                        nc.gpsimd.tensor_scalar(xn2[:, j], xn[:, j], r2[:, j:j + 1], 1.0, ALU.mult, ALU.mult).then_inc(s_xn2, 1)

                norms(0)
                second(0, True)
                nc.gpsimd.memset(v_all[:, :, :, 2 * DH:VW], 1.0).then_inc(s_ones, 1)

                def body(g, it, u, more):
                    if more:
                        norms(g + 1)
                        second(g + 1, False)
                    for i in range(QK_PER):
                        pool.wait_ge(s_pa, g * PJ_PER + (RING + i + 1))
                        pool.wait_ge(st_qk[i % RING], g * (32 * QK_PER // RING) + (32 * (i // RING) + 32))
                        bare(pool, s_bare)
                        nc.gpsimd.tensor_scalar(qk_head[:, i % RING], qk32[:, i % RING], 1.0, 0.0, ALU.mult, ALU.add).then_inc(s_ph, 1)
                groups(pool, body)

            @block.scalar
            def _(act):
                act.sem_inc(s_pa, RING)

                def head(g, i, it, u):
                    act.wait_ge(s_t, g * T_PER + (i + 1))
                    if i == 0:
                        act.wait_ge(st_xf[u], it * 64 + 64)
                    dst = f_head if i % 2 == 0 else a_head
                    nc.scalar.activation(dst[:, u, :, P * (i // 2):P * (i // 2 + 1)],
                                         tps[:, i % RING].rearrange("p (k n) -> p k n", k=KT), ACT.Copy).then_inc(s_th, 1)

                for i in range(T_PER):
                    head(0, i, 0, 0)

                def body(g, it, u, more):
                    for i in range(PJ_PER):
                        if more and i < T_PER:
                            head(g + 1, i, *nxt(it, u))
                        act.wait_ge(s_pj, g * PJ_PER + (i + 1))
                        if i < QK_PER:
                            act.wait_ge(s_pt, g * PJ_PER + (i + 1))
                            m, mt = divmod(i, KT)
                            nc.scalar.activation(qk32[:, i % RING], pjs[:, i % RING], ACT.Identity,
                                                 scale=kept["unscale"][:, m:m + 1],
                                                 bias=kept["qk_bias"][:, m, mt:mt + 1]).then_inc(s_pa, 1)
                        else:
                            nc.scalar.activation(v_all[:, H * u:H * (u + 1), bass.ds(it * JT + (i - QK_PER), 1), 0:DH],
                                                 pjs[:, i % RING].rearrange("p (h a d) -> p h a d", a=1, h=H), ACT.Copy,
                                                 scale=V_SHIFT).then_inc(s_pa, 1)
                groups(act, body)

            @block.vector
            def _(dve):
                dve.sem_inc(s_pt, RING)

                def norms(g, it, u, first):
                    own = Steps(dve, s_own, g * OWN_PER)
                    dve.wait_ge(ld_x[u], it * 16 + 16)
                    for j in range(JT):
                        own.did(nc.vector.bn_stats(st6[:, j], xin[:, u, j]))
                    own.settle()
                    bare(dve, s_bare)
                    for j in range(JT):
                        own.did(nc.vector.bn_aggr(mv[:, j], st6[:, j]))
                    own.settle()
                    nc.vector.tensor_scalar(va[:], mv[:, :, 1], EPS, None, ALU.add).then_inc(s_va, 1)
                    dve.wait_ge(s_r1, g + 1)
                    for j in range(JT):
                        if not first:
                            dve.wait_ge(s_t, g * T_PER + (2 * j + 1 - T_PER))
                            dve.wait_ge(s_xn2, g * JT + (j + 1 - JT))
                        nc.vector.tensor_scalar(xn[:, j], xin[:, u, j], mv[:, j, 0:1], r1[:, j:j + 1],
                                                ALU.subtract, ALU.mult).then_inc(s_xn, 1)
                        if j == 0:
                            own.did(nc.vector.tensor_tensor(vb[:], mv[:, :, 1], r1[:], ALU.mult))
                            own.settle()
                            own.did(nc.vector.tensor_tensor(vc[:], vb[:], r1[:], ALU.mult))
                            own.settle()
                            nc.vector.tensor_scalar(vd[:], vc[:], EPS, None, ALU.add).then_inc(s_vd, 1)
                    assert own.n == OWN_PER

                def tail(g, i, u):
                    dve.wait_ge(s_th, g * T_PER + (i + 1))
                    hi, lo = (f_head, f_tail) if i % 2 == 0 else (a_head, a_tail)
                    c = slice(P * (i // 2), P * (i // 2 + 1))
                    nc.vector.tensor_tensor(lo[:, u, :, c], tps[:, i % RING].rearrange("p (k n) -> p k n", k=KT),
                                            hi[:, u, :, c], ALU.subtract).then_inc(s_tt, 1)

                norms(0, 0, 0, True)
                for i in range(T_PER):
                    tail(0, i, 0)

                def body(g, it, u, more):
                    if more:
                        norms(g + 1, *nxt(it, u), False)
                    for i in range(PJ_PER):
                        if more and i < T_PER:
                            tail(g + 1, i, nxt(it, u)[1])
                        if i < QK_PER:
                            dve.wait_ge(s_ph, g * QK_PER + (i + 1))
                            nc.vector.tensor_tensor(qk_tail[:, i % RING], qk32[:, i % RING], qk_head[:, i % RING],
                                                    ALU.subtract).then_inc(s_pt, 1)
                        else:
                            dve.wait_ge(s_pa, g * PJ_PER + (RING + i + 1))
                            vt = v_all[:, H * u:H * (u + 1), bass.ds(it * JT + (i - QK_PER), 1), :].rearrange("p h a d -> p (h a) d")
                            nc.vector.scalar_tensor_tensor(vt[:, :, DH:2 * DH], pjs[:, i % RING].rearrange("p (h d) -> p h d", h=H),
                                                           V_SHIFT, vt[:, :, 0:DH], ALU.mult, ALU.subtract).then_inc(s_pt, 1)
                groups(dve, body)

            @block.tensor
            def _(pe):
                def transpose(g, i, first):
                    j = i // 2
                    pe.wait_ge(s_xn if i % 2 == 0 else s_xn2, g * JT + (j + 1))
                    if not (first and i < RING):
                        pe.wait_ge(s_tt, g * T_PER + (i + 1 - RING))
                    src = xn if i % 2 == 0 else xn2
                    for k in range(KT):
                        last = nc.tensor.transpose(tps[:, i % RING, k * P:(k + 1) * P], src[:, j, k * P:(k + 1) * P],
                                                   kept["ident32"][:])
                    last.then_inc(s_t, 1)

                for i in range(T_PER):
                    transpose(0, i, True)

                wh, wt = kept["w_head"], kept["w_tail"]

                def body(g, it, u, more):
                    pe.wait_ge(s_tt, g * T_PER + T_PER)
                    for i in range(PJ_PER):
                        pe.wait_ge(s_pa, g * PJ_PER + (i + 1))
                        pe.wait_ge(s_pt, g * PJ_PER + (i + 1))
                        m, mt = divmod(i, KT)
                        for k in range(KT):
                            ws = slice(mt * P, (mt + 1) * P)
                            if m < V:
                                pairs = [(wh[:, m, k, ws], a_head[:, u, k]), (wh[:, m, k, ws], a_tail[:, u, k]),
                                         (wt[:, m, k, ws], a_head[:, u, k])]
                            else:
                                pairs = [(a_head[:, u, k, ws], wh[:, m, k]), (a_head[:, u, k, ws], wt[:, m, k]),
                                         (a_tail[:, u, k, ws], wh[:, m, k])]
                            for n, (a, b) in enumerate(pairs):
                                last = nc.tensor.matmul(pjs[:, i % RING], a, b, start=(k == 0 and n == 0),
                                                        stop=(k == KT - 1 and n == 2))
                        last.then_inc(s_pj, 1)
                        if more and i < T_PER:
                            transpose(g + 1, i, False)
                groups(pe, body)


QB = S // P
NG = S // G
LAG = 5
HEAD_LAG = LAG - 1
TAIL_LAG = LAG - 2
SHIFT = 8
MX_LEAD = 28
P_SHIFT = 10
SCALE = DH ** -0.5
FT = 2 * P


def attention_steps():
    steps = []
    for g in range(NG):
        for j in range(0, JT * (g + 1), 2):
            parts, at = [], 0
            for key in (j, j + 1):
                q0 = max(0, key - JT * g) * P
                parts.append((key, q0, at))
                at += G - q0
            steps.append((g, parts, at))
    return steps


def maximum_rounds():
    rounds = [[(0, 0, P, 0, 0), (1, 0, 2 * P, G, 0)], [(2, 0, 3 * P, 0, 0), (3, 0, 4 * P, G, 0)]]
    rounds += [[(i, 0, min(i + 1, 8) * P, 0, 0)] for i in range(4, QB)]
    rounds += [[(8, 2 * G, P, 0, 1), (9, 2 * G, 2 * P, G, 1)], [(10, 2 * G, 3 * P, 0, 1), (11, 2 * G, 4 * P, G, 1)]]
    rounds += [[(i, 2 * G, (i - 7) * P, 0, 1)] for i in range(12, QB)]
    return rounds


STEPS, ROUNDS = attention_steps(), maximum_rounds()
NS = len(STEPS)
assert len(ROUNDS) == NS
MX_USES = NS + 1
HEAD_BY_ACT = [s for s in range(NS) if s % 5 in (0, 2, 4)]
TAIL_BY_POOL = [s for s in range(NS) if s % 5 in (1, 3)]
HEAD_BY_POOL = [s for s in range(NS) if s not in HEAD_BY_ACT]
TAIL_BY_DVE = [s for s in range(NS) if s not in TAIL_BY_POOL]
F1_AT = {1 + 2 * m: m for m in range(HT)}
F2_AT = {22 + c: (0, c) for c in range(5)} | {30 + c: (1, c) for c in range(5)}


def attend_block(nc, qk_dram, xf_dram, gate_dram, kept):
    with ExitStack() as ctx:
        def sb(name, shape, dt):
            return ctx.enter_context(nc.sbuf_tensor(name, shape, dt))

        def sem(name):
            return ctx.enter_context(nc.semaphore(name))

        q_mx = [sb(f"q_mx{u}", [P, S], F16) for u in range(2)]
        k_mx = [sb(f"k_mx{u}", [P, S], F16) for u in range(2)]
        q_st = [sb(f"q_st{u}", [P, S], F16) for u in range(2)]
        k_st = [sb(f"k_st{u}", [P, S], F16) for u in range(2)]
        w32 = sb("w32", [P, 4, 2 * G], F32)
        w_hd = sb("w_hd", [P, 8, 2 * G], F16)
        w_tl = sb("w_tl", [P, 5, 2 * G], F16)
        v_st = sb("v_st", [P, 2, QB, VW], F16)
        mx = sb("mx", [P, 2, QB], F32)
        mm = sb("mm", [P, QB], F32)
        mneg = sb("mneg", [P, QB], F32)
        m_ht = sb("m_ht", [P, 2, QB], F16)
        m_rows = sb("m_rows", [2 * QB, P], F16)
        o_raw = sb("o_raw", [P, 2, QB, VW], F32)
        rden = sb("rden", [P, QB], F32)
        xf = sb("xf", [P, 2, KT, FT], F16)
        r32 = sb("r32", [P, 2, FT], F32)
        s32 = sb("s32", [P, 2, FT], F32)
        s_hd = sb("s_hd", [P, HT, FT], F16)
        s_tl = sb("s_tl", [P, HT, FT], F16)
        e32 = sb("e32", [P, D], F32)
        g32 = sb("g32", [P, 2, D], F32)
        st_ps = ctx.enter_context(nc.psum_tensor("st_ps", [P, 2, 2 * G], F32))
        mx_ps = ctx.enter_context(nc.psum_tensor("mx_ps", [P, 2 * G], F32))
        av_ps = ctx.enter_context(nc.psum_tensor("av_ps", [P, G], F32))
        ff_ps = ctx.enter_context(nc.psum_tensor("ff_ps", [P, D], F32))
        av = av_ps[:, 0:JT * VW].rearrange("p (i v) -> p i v", i=JT)
        v_all = kept["v_all"]

        ld_mx = [sem(f"ld_mx{u}") for u in range(2)]
        ld_st = [sem(f"ld_st{u}") for u in range(2)]
        ld_mr = [sem(f"ld_mr{u}") for u in range(2)]
        ld_xf = sem("ld_xf")
        st_g = [sem(f"st_g{u}") for u in range(2)]
        s_set = sem("s_set")
        s_st = sem("s_st")
        s_exp = sem("s_exp")
        s_hda = sem("s_hda")
        s_hdp = sem("s_hdp")
        s_tld = sem("s_tld")
        s_tlp = sem("s_tlp")
        s_av = sem("s_av")
        s_avc = sem("s_avc")
        s_vs = sem("s_vs")
        s_mx = sem("s_mx")
        s_mr = sem("s_mr")
        s_m = sem("s_m")
        s_mh = sem("s_mh")
        s_rd = sem("s_rd")
        s_os = sem("s_os")
        s_on = sem("s_on")
        s_oh = sem("s_oh")
        s_ot = sem("s_ot")
        s_f1 = sem("s_f1")
        s_re = sem("s_re")
        s_sq = sem("s_sq")
        s_sh = sem("s_sh")
        s_sl = sem("s_sl")
        s_f2 = sem("s_f2")
        s_e = sem("s_e")
        s_ga = sem("s_ga")
        s_bare = sem("s_bare_a")

        PAIRS = UNITS // 2
        N2 = 2 * NS

        def place(it, n):
            return it * 2 + n // NS, (n // NS) % 2, it + n // N2, n % NS

        def nth(which, unit, s):
            while s < 0:
                unit, s = unit - 1, s + NS
            return unit * len(which) + sum(x <= s for x in which)

        def tail_done(eng, unit, s):
            while s < 0:
                unit, s = unit - 1, s + NS
            if s in TAIL_BY_POOL:
                eng.wait_ge(s_tlp, nth(TAIL_BY_POOL, unit, s))
            else:
                eng.wait_ge(s_tld, nth(TAIL_BY_DVE, unit, s))

        def head_done(eng, unit, s):
            if s in HEAD_BY_ACT:
                eng.wait_ge(s_hda, nth(HEAD_BY_ACT, unit, s))
            else:
                eng.wait_ge(s_hdp, nth(HEAD_BY_POOL, unit, s))

        def exists(it, n):
            return not (isinstance(it, int) and it * N2 + n >= UNITS * NS)

        def before(it, n, k):
            return isinstance(it, int) and it * N2 + n < k

        def pairs(eng, body):
            with eng.Fori(0, PAIRS - 1) as it:
                body(it)
            body(PAIRS - 1)

        def all_steps(eng, step):
            for n in range(SHIFT):
                step(0, n)
            with eng.Fori(0, PAIRS - 1) as it:
                for n in range(SHIFT, SHIFT + N2):
                    step(it, n)
            for n in range(SHIFT, N2):
                step(PAIRS - 1, n)

        with nc.Block() as block:
            @block.sync
            def _(sp):
                for u in range(2):
                    sp.sem_inc(st_g[u], 16)

                def load_operands(unit, q_to, k_to, semaphore):
                    src = qk_dram[bass.ds(unit, 1)]
                    hd_tl = lambda m: src[:, m].rearrange("a t d s -> (a t d) s")
                    hd = lambda m: src[:, m, 0].rearrange("a d s -> (a d) s")
                    sp.dma_start(q_to[0:64, :], hd_tl(0)).then_inc(semaphore, 16)
                    sp.dma_start(q_to[64:96, :], hd(0)).then_inc(semaphore, 16)
                    sp.dma_start(k_to[0:32, :], hd(1)).then_inc(semaphore, 16)
                    sp.dma_start(k_to[32:96, :], hd_tl(1)).then_inc(semaphore, 16)

                def store_rows(unit, u):
                    sp.wait_ge(s_mr, unit * MX_USES + (MX_USES + 1))
                    for t in range(2):
                        sp.dma_start(q_st[u][96 + t:97 + t, :].rearrange("a (i c) -> a i c", i=QB),
                                     m_rows[QB * t:QB * (t + 1), :]).then_inc(ld_mr[u], 16)

                load_operands(0, q_mx[0], k_mx[0], ld_mx[0])
                load_operands(1, q_mx[1], k_mx[1], ld_mx[1])
                load_operands(0, q_st[0], k_st[0], ld_st[0])
                sp.dma_start(xf[:], xf_dram[0]).then_inc(ld_xf, 16)
                store_rows(0, 0)

                def store_gates(it):
                    for t in range(2):
                        sp.wait_ge(s_ga, it * 2 + (t + 2))
                        sp.dma_start(gate_dram[bass.ds(it * 2 + t, 1)].rearrange("a p d -> (a p) d"), g32[:, t]).then_inc(st_g[t], 16)

                def body(it):
                    last = isinstance(it, int)
                    for u in range(2):
                        unit = it * 2 + u
                        if not last:
                            load_operands(unit + 2, q_mx[u], k_mx[u], ld_mx[u])
                        if not (last and u == 1):
                            sp.wait_ge(s_st, unit * NS + 1)
                            load_operands(unit + 1, q_st[1 - u], k_st[1 - u], ld_st[1 - u])
                            store_rows(unit + 1, 1 - u)
                        if not last and u == 0:
                            sp.wait_ge(s_f1, it * HT + HT)
                            sp.dma_start(xf[:], xf_dram[bass.ds(it + 1, 1)].rearrange("a p t k n -> (a p) t k n")).then_inc(ld_xf, 16)
                    store_gates(it)
                pairs(sp, body)
                for t in range(2):
                    sp.wait_ge(st_g[t], 16 + 16 * PAIRS)

            @block.tensor
            def _(pe):
                pe.sem_inc(s_st, 1)
                pe.sem_inc(s_av, 4)
                pe.sem_inc(s_f2, 1)

                def scores(it, n):
                    unit, u, nth_pair, s = place(it, n)
                    g, parts, _ = STEPS[s]
                    if s == 0:
                        pe.wait_ge(ld_st[u], nth_pair * 64 + 64)
                        pe.wait_ge(ld_mr[u], nth_pair * 32 + 32)
                    if not before(it, n, 2):
                        pe.wait_ge(s_exp, unit * NS + (s - 1))
                    for key, q0, at in parts:
                        out = st_ps[:, n % 2, at:at + G - q0]
                        kt = k_st[u][0:98, key * P:(key + 1) * P]
                        diagonal = key >= JT * g
                        last = nc.tensor.matmul(out, kt, q_st[u][0:98, g * G + q0:(g + 1) * G], start=True, stop=not diagonal)
                        if diagonal:
                            last = nc.tensor.matmul(out[:, 0:P], kept["identb"][:], kept["mask_kq"][:], start=False, stop=True)
                    last.then_inc(s_st, 1)

                def maxima(unit, u, nth_pair, r):
                    if r == 0:
                        pe.wait_ge(ld_mx[u], nth_pair * 64 + 64)
                    pe.wait_ge(s_mr, unit * MX_USES + (r + 1))
                    for i, k0, w, col, _ in ROUNDS[r]:
                        for c in range(0, w, G):
                            cw = min(G, w - c)
                            out = mx_ps[:, col + c:col + c + cw]
                            diagonal = k0 + c + cw == (i + 1) * P
                            last = nc.tensor.matmul(out, q_mx[u][0:96, i * P:(i + 1) * P], k_mx[u][0:96, k0 + c:k0 + c + cw],
                                                    start=True, stop=not diagonal)
                            if diagonal:
                                last = nc.tensor.matmul(out[:, cw - P:cw], kept["identb"][:], kept["mask_qk"][:],
                                                        start=False, stop=True)
                    last.then_inc(s_mx, 1)

                def transpose_maxima(unit):
                    pe.wait_ge(s_mh, unit + 1)
                    pe.wait_ge(s_mr, unit * MX_USES + (NS + 1))
                    nc.tensor.transpose(mx_ps[0:2 * QB, 0:P // 2].bitcast(F16), m_ht[:].rearrange("p t i -> p (t i)"),
                                        kept["ident16"][:]).then_inc(s_mx, 1)

                def weighted(it, n):
                    unit, u, _, s = place(it, n)
                    g, parts, _ = STEPS[s]
                    if s == 0:
                        pe.wait_ge(s_vs, unit + 1)
                    if parts[0][0] == 0:
                        pe.wait_ge(s_avc, unit * NG + (g + 1))
                    tail_done(pe, unit, s)
                    for key, q0, at in parts:
                        for w in (w_hd, w_tl):
                            for i in range(q0 // P, JT):
                                c = at + i * P - q0
                                last = nc.tensor.matmul(av[:, i], w[:, n % (8 if w is w_hd else 5), c:c + P], v_st[:, u, key],
                                                        start=(key == 0 and w is w_hd and i == 0),
                                                        stop=(key == JT * g + JT - 1 and w is w_tl and i == JT - 1),
                                                        skip_group_check=True)
                    last.then_inc(s_av, 1)

                def hidden(it, m):
                    if m == 0:
                        pe.wait_ge(ld_xf, it * 16 + 16)
                        pe.wait_ge(s_ga, it * 2 + 1)
                    else:
                        pe.wait_ge(s_re, it * HT + m)
                    for k in range(KT):
                        for t in range(2):
                            last = nc.tensor.matmul(ff_ps[:, 0:FT], kept["fc_T"][:, k, m * P:(m + 1) * P], xf[:, t, k],
                                                    start=(k == 0 and t == 0), stop=(k == KT - 1 and t == 1))
                    last.then_inc(s_f1, 1)

                def outward(it, t, c):
                    if c == 0:
                        if t == 0:
                            pe.wait_ge(s_re, it * HT + HT)
                            pe.wait_ge(s_sl, it * HT + (HT + 2))
                        else:
                            pe.wait_ge(s_ga, it * 2 + 2)
                    for m in (2 * c, 2 * c + 1):
                        for w in (s_hd, s_tl):
                            last = nc.tensor.matmul(ff_ps[:], w[:, m, t * P:(t + 1) * P], kept["proj_T"][:, m],
                                                    start=(m == 0 and w is s_hd), stop=(m == HT - 1 and w is s_tl))
                    if c == 4:
                        last.then_inc(s_f2, 1)

                for r in range(NS):
                    maxima(0, 0, 0, r)
                transpose_maxima(0)
                pe.wait_ge(s_set, 3)
                for r in range(MX_LEAD - NS):
                    maxima(1, 1, 0, r)
                    if r < LAG:
                        scores(0, r)

                def step(it, n):
                    pair, m = it + n // N2, n % N2
                    if exists(it, n + LAG):
                        scores(it, n + LAG)
                    if exists(it, n + MX_LEAD - 1) and (n + MX_LEAD) % NS == 0:
                        transpose_maxima(place(it, n + MX_LEAD - 1)[0])
                    if exists(it, n + MX_LEAD):
                        maxima(*place(it, n + MX_LEAD))
                    if m in F1_AT:
                        hidden(pair, F1_AT[m])
                    if m in F2_AT:
                        outward(pair, *F2_AT[m])
                    weighted(it, n)
                all_steps(pe, step)

            @block.scalar
            def _(act):
                act.sem_inc(s_avc, 1)

                def weights(it, n):
                    unit, u, _, s = place(it, n)
                    cols = STEPS[s][2]
                    act.wait_ge(s_st, unit * NS + (s + 2))
                    if not before(it, n, 4):
                        tail_done(act, unit, s - 4)
                    nc.scalar.activation(w32[:, n % 4, 0:cols], st_ps[:, n % 2, 0:cols], ACT.Exp, scale=SCALE).then_inc(s_exp, 1)

                def heads(it, n):
                    unit, u, _, s = place(it, n)
                    cols = STEPS[s][2]
                    if not before(it, n, 8):
                        act.wait_ge(s_av, unit * NS + (s - 3))
                    nc.scalar.activation(w_hd[:, n % 8, 0:cols], st_ps[:, n % 2, 0:cols], ACT.Exp, scale=SCALE).then_inc(s_hda, 1)

                def front(it, n):
                    unit, u, _, s = place(it, n)
                    if s in HEAD_BY_ACT:
                        act.wait_ge(s_st, unit * NS + (s + 2))
                        heads(it, n)
                    weights(it, n)

                def copy_out(it, n):
                    unit, u, _, s = place(it, n)
                    g = STEPS[s][0]
                    act.wait_ge(s_av, unit * NS + (s + 5))
                    if g == 0:
                        act.wait_ge(s_ot, unit + 1)
                    nc.scalar.activation(o_raw[:, u, JT * g:JT * (g + 1)], av, ACT.Copy).then_inc(s_avc, 1)

                def relu(it, m):
                    act.wait_ge(s_f1, it * HT + (m + 1))
                    act.wait_ge(s_sq, it * HT + (m + 1))
                    nc.scalar.activation(r32[:, m % 2], ff_ps[:, 0:FT], ACT.Relu, scale=0.25).then_inc(s_re, 1)

                def gate_tanh(it, t):
                    act.wait_ge(s_f2, it * 2 + (t + 2))
                    act.wait_ge(s_ga, it * 2 + (t + 1))
                    nc.scalar.activation(e32[:], ff_ps[:], ACT.Tanh, scale=kept["ffn_scale"][:]).then_inc(s_e, 1)

                for n in range(LAG):
                    front(0, n)

                def step(it, n):
                    pair, m, s = it + n // N2, n % N2, n % NS
                    if exists(it, n + LAG):
                        front(it, n + LAG)
                    if m in F1_AT:
                        relu(pair, F1_AT[m])
                    if m in F2_AT and F2_AT[m][1] == 4:
                        gate_tanh(pair, F2_AT[m][0])
                    if s == NS - 1 or STEPS[s + 1][0] != STEPS[s][0]:
                        copy_out(it, n)
                all_steps(act, step)

            @block.gpsimd
            def _(pool):
                pool.sem_inc(s_sq, 2)
                pool.sem_inc(s_sl, 2)

                def head(it, n):
                    unit, u, _, s = place(it, n)
                    if s not in HEAD_BY_POOL:
                        return
                    cols = STEPS[s][2]
                    pool.wait_ge(s_exp, unit * NS + (s + 1))
                    if not before(it, n, 8):
                        pool.wait_ge(s_av, unit * NS + (s - 3))
                    bare(pool, s_bare)
                    nc.gpsimd.tensor_scalar(w_hd[:, n % 8, 0:cols], w32[:, n % 4, 0:cols], 1.0, 0.0, ALU.mult, ALU.add).then_inc(s_hdp, 1)

                def tail(it, n):
                    unit, u, _, s = place(it, n)
                    if s not in TAIL_BY_POOL:
                        return
                    cols = STEPS[s][2]
                    pool.wait_ge(s_exp, unit * NS + (s + 1))
                    head_done(pool, unit, s)
                    if not before(it, n, 5):
                        pool.wait_ge(s_av, unit * NS + s)
                    nc.gpsimd.tensor_tensor(w_tl[:, n % 5, 0:cols], w32[:, n % 4, 0:cols], w_hd[:, n % 8, 0:cols],
                                            ALU.subtract).then_inc(s_tlp, 1)

                def square(it, m):
                    pool.wait_ge(s_sl, it * HT + (m + 1))
                    pool.wait_ge(s_re, it * HT + (m + 1))
                    if m == 0:
                        pool.wait_ge(s_f2, it * 2 + 1)
                    nc.gpsimd.tensor_tensor(s32[:, m % 2], r32[:, m % 2], r32[:, m % 2], ALU.mult).then_inc(s_sq, 1)
                    pool.wait_ge(s_sq, it * HT + (m + 3))
                    bare(pool, s_bare)
                    nc.gpsimd.tensor_scalar(s_hd[:, m], s32[:, m % 2], 1.0, 0.0, ALU.mult, ALU.add).then_inc(s_sh, 1)
                    pool.wait_ge(s_sh, it * HT + (m + 1))
                    nc.gpsimd.tensor_tensor(s_tl[:, m], s32[:, m % 2], s_hd[:, m], ALU.subtract).then_inc(s_sl, 1)

                def normalise(unit, u):
                    pool.wait_ge(s_rd, unit + 1)
                    o = o_raw[:, u, :, 0:DH]
                    nc.gpsimd.tensor_tensor(o, o, o_raw[:, u, :, DH:2 * DH], ALU.add).then_inc(s_os, 1)
                    pool.wait_ge(s_os, unit + 1)
                    nc.gpsimd.tensor_tensor(o, o, rden[:].rearrange("p (i a) -> p i a", a=1).to_broadcast([P, QB, DH]),
                                            ALU.mult).then_inc(s_on, 1)

                for n in range(HEAD_LAG):
                    head(0, n)
                    if n < TAIL_LAG:
                        tail(0, n)

                def step(it, n):
                    pair, m, s = it + n // N2, n % N2, n % NS
                    if exists(it, n + TAIL_LAG):
                        tail(it, n + TAIL_LAG)
                    if exists(it, n + HEAD_LAG):
                        head(it, n + HEAD_LAG)
                    if m in F1_AT:
                        square(pair, F1_AT[m])
                    if s == 2 and not before(it, n, NS):
                        unit, u, _, _ = place(it, n)
                        normalise(unit - 1, 1 - u)
                all_steps(pool, step)
                normalise(UNITS - 1, 1)

            @block.vector
            def _(dve):
                dve.sem_inc(s_mr, 1)
                dve.sem_inc(s_ot, 2)
                dve.sem_inc(s_ga, 1)
                nc.vector.memset(mx[:, 1, 0:QB // 2], -BIG).then_inc(s_set, 1)
                for k in k_st:
                    nc.vector.memset(k[96:98, :], 256.0).then_inc(s_set, 1)
                dve.wait_ge(s_set, 3)

                def reduce(unit, u, nth_pair, r):
                    dve.wait_ge(s_mx, unit * MX_USES + (r + 1))
                    for x, (i, k0, w, col, half) in enumerate(ROUNDS[r]):
                        last = nc.vector.tensor_reduce(mx[:, half, i:i + 1], mx_ps[:, col:col + w], AX.X, ALU.max)
                    last.then_inc(s_mr, 1)

                def split_maxima(unit):
                    dve.wait_ge(s_mr, unit * MX_USES + (NS + 1))
                    nc.vector.tensor_tensor(mm[:], mx[:, 0], mx[:, 1], ALU.max).then_inc(s_m, 1)
                    dve.wait_ge(s_m, unit * 3 + 1)
                    nc.vector.tensor_scalar(mneg[:], mm[:], -1.0 / 256, float(P_SHIFT * np.log(2.0) / SCALE / 256),
                                            ALU.mult, ALU.add).then_inc(s_m, 1)
                    dve.wait_ge(s_m, unit * 3 + 2)
                    nc.vector.tensor_copy(m_ht[:, 0], mneg[:]).then_inc(s_m, 1)
                    dve.wait_ge(s_m, unit * 3 + 3)
                    nc.vector.tensor_tensor(m_ht[:, 1], mneg[:], m_ht[:, 0], ALU.subtract).then_inc(s_mh, 1)

                def copy_rows(unit, u, nth_pair):
                    dve.wait_ge(s_mx, unit * MX_USES + MX_USES)
                    if not (isinstance(unit, int) and unit == 0):
                        v, p = (1 - u), (nth_pair if u == 1 else nth_pair - 1)
                        dve.wait_ge(ld_mr[v], p * 32 + 32)
                    nc.vector.tensor_copy(m_rows[:], mx_ps[0:2 * QB, 0:P // 2].bitcast(F16)).then_inc(s_mr, 1)

                def place_v(unit, u):
                    bare(dve, s_bare)
                    nc.vector.tensor_copy(v_st[:, u], v_all[:, bass.ds(unit, 1)].rearrange("p a i v -> p (a i) v")).then_inc(s_vs, 1)

                def tail(it, n):
                    unit, u, _, s = place(it, n)
                    if s not in TAIL_BY_DVE:
                        return
                    cols = STEPS[s][2]
                    dve.wait_ge(s_exp, unit * NS + (s + 1))
                    head_done(dve, unit, s)
                    if not before(it, n, 5):
                        dve.wait_ge(s_av, unit * NS + s)
                    nc.vector.tensor_tensor(w_tl[:, n % 5, 0:cols], w32[:, n % 4, 0:cols], w_hd[:, n % 8, 0:cols],
                                            ALU.subtract).then_inc(s_tld, 1)

                def reciprocals(unit, u):
                    dve.wait_ge(s_avc, unit * NG + (NG + 1))
                    nc.vector.reciprocal(rden[:], o_raw[:, u, :, 2 * DH]).then_inc(s_rd, 1)

                def split_output(unit, u):
                    dve.wait_ge(s_on, unit + 1)
                    at = v_all[:, bass.ds(unit, 1)].rearrange("p a i v -> p (a i) v")
                    o = o_raw[:, u, :, 0:DH]
                    bare(dve, s_bare)
                    nc.vector.tensor_copy(at[:, :, 0:DH], o).then_inc(s_oh, 1)
                    dve.wait_ge(s_oh, unit + 1)
                    nc.vector.tensor_tensor(at[:, :, DH:2 * DH], o, at[:, :, 0:DH], ALU.subtract).then_inc(s_ot, 1)

                def gate(it, t):
                    dve.wait_ge(s_e, it * 2 + (t + 1))
                    dve.wait_ge(st_g[t], it * 16 + 16)
                    nc.vector.scalar_tensor_tensor(g32[:, t], e32[:], 1.0, ff_ps[:], ALU.add, ALU.mult).then_inc(s_ga, 1)

                for r in range(NS):
                    reduce(0, 0, 0, r)
                split_maxima(0)
                copy_rows(0, 0, 0)
                place_v(0, 0)
                for r in range(MX_LEAD - NS):
                    reduce(1, 1, 0, r)
                    if r < TAIL_LAG:
                        tail(0, r)

                def step(it, n):
                    pair, m, s = it + n // N2, n % N2, n % NS
                    unit, u, _, _ = place(it, n)
                    if exists(it, n + MX_LEAD - 1) and (n + MX_LEAD) % NS == 0:
                        copy_rows(*place(it, n + MX_LEAD - 1)[:3])
                    if exists(it, n + MX_LEAD):
                        reduce(*place(it, n + MX_LEAD))
                        if (n + MX_LEAD) % NS == NS - 1:
                            split_maxima(place(it, n + MX_LEAD)[0])
                    if exists(it, n + TAIL_LAG):
                        tail(it, n + TAIL_LAG)
                    if s == 10 and exists(it, n + NS):
                        dve.wait_ge(s_av, unit * NS + 4)
                        place_v(unit + 1, 1 - u)
                    if m in F2_AT and F2_AT[m][1] == 4:
                        gate(pair, F2_AT[m][0])
                    if not before(it, n, NS):
                        if s == 1:
                            reciprocals(unit - 1, 1 - u)
                        if s == 4:
                            split_output(unit - 1, 1 - u)
                all_steps(dve, step)
                reciprocals(UNITS - 1, 1)
                split_output(UNITS - 1, 1)


def finish_block(nc, x, out, gate_dram, kept):
    with ExitStack() as ctx:
        def sb(name, shape, dt):
            return ctx.enter_context(nc.sbuf_tensor(name, shape, dt))

        def sem(name):
            return ctx.enter_context(nc.semaphore(name))

        xt = sb("xt", [P, 2, D], F32)
        gt = sb("gt", [P, 2, D], F32)
        og = sb("og", [P, 2, 2, D], F16)
        oT = sb("oT", [P, 2, 2, KT, P], F16)
        y1 = sb("y1", [P, 2, D], F32)
        y2 = sb("y2", [P, 2, D], F32)
        y3 = sb("y3", [P, 2, D], F32)
        tps = ctx.enter_context(nc.psum_tensor("o_tp", [P, 2, 2, D], F16))
        pso = ctx.enter_context(nc.psum_tensor("o_pj", [P, 2, D], F32))
        v_all = kept["v_all"]

        ld = [sem(f"ld_t{t}") for t in range(2)]
        st = [sem(f"st_t{t}") for t in range(2)]
        s_bare = sem("s_bare_f")
        s_g = sem("s_og")
        s_t, s_c = sem("s_ot_t"), sem("s_ot_c")
        s_p = sem("s_op")
        s_y1, s_y2, s_y3 = sem("s_y1"), sem("s_y2"), sem("s_y3")

        with nc.Block() as block:
            @block.sync
            def _(sp):
                for t in range(2):
                    sp.sem_inc(st[t], 16)
                with sp.Fori(0, QB) as i:
                    for t in range(2):
                        sp.wait_ge(s_y3, i * 2 + (t + 1))
                        sp.dma_start(xt[:, t], x[t, bass.ds(i * P, P), :]).then_inc(ld[t], 16)
                        sp.dma_start(gt[:, t], gate_dram[bass.ds(i + QB * t, 1)].rearrange("a p d -> (a p) d")).then_inc(ld[t], 16)

            @block.tensor
            def _(pe):
                pe.sem_inc(s_p, 2)
                pe.sem_inc(s_t, 2)
                with pe.Fori(0, QB) as i:
                    for t in range(2):
                        pe.wait_ge(s_g, i * 2 + (t + 1))
                        pe.wait_ge(s_c, i * 2 + (t + 1))
                        for part in range(2):
                            for k in range(KT):
                                last = nc.tensor.transpose(tps[:, t, part, k * P:(k + 1) * P], og[:, t, part, k * P:(k + 1) * P],
                                                           kept["ident16"][:])
                        last.then_inc(s_t, 1)
                    for t in range(2):
                        pe.wait_ge(s_c, i * 2 + (t + 3))
                        pe.wait_ge(s_y1, i * 2 + (t + 1))
                        for k in range(KT):
                            for n, (a, b) in enumerate(((0, "wo_head"), (0, "wo_tail"), (1, "wo_head"))):
                                last = nc.tensor.matmul(pso[:, t], oT[:, t, a, k], kept[b][:, k],
                                                        start=(k == 0 and n == 0), stop=(k == KT - 1 and n == 2))
                        last.then_inc(s_p, 1)

            @block.scalar
            def _(act):
                act.sem_inc(s_c, 2)
                with act.Fori(0, QB) as i:
                    for t in range(2):
                        act.wait_ge(s_t, i * 2 + (t + 3))
                        act.wait_ge(s_p, i * 2 + (t + 1))
                        nc.scalar.activation(oT[:, t].rearrange("p a k n -> p (a k n)"), tps[:, t].rearrange("p a n -> p (a n)"),
                                             ACT.Copy).then_inc(s_c, 1)
                    for t in range(2):
                        act.wait_ge(s_y3, i * 2 + (t + 3))
                        act.dma_start(out[t, bass.ds(i * P, P), :], y3[:, t]).then_inc(st[t], 16)
                for t in range(2):
                    act.wait_ge(st[t], 16 + 16 * QB)

            @block.vector
            def _(dve):
                dve.sem_inc(s_y1, 2)
                dve.sem_inc(s_y3, 2)
                with dve.Fori(0, QB) as i:
                    for t in range(2):
                        dve.wait_ge(s_t, i * 2 + (t + 1))
                        bare(dve, s_bare)
                        for part in range(2):
                            heads = v_all[:, H * t:H * (t + 1), bass.ds(i, 1), DH * part:DH * (part + 1)]
                            last = nc.vector.tensor_copy(og[:, t, part].rearrange("p (h d) -> p h d", h=H),
                                                         heads.rearrange("p h a d -> p (h a) d"))
                        last.then_inc(s_g, 1)
                    for t in range(2):
                        dve.wait_ge(s_p, i * 2 + (t + 3))
                        nc.vector.scalar_tensor_tensor(y1[:, t], pso[:, t], kept["out_scale"][:], kept["out_bias"][:],
                                                       ALU.mult, ALU.add).then_inc(s_y1, 1)
                        dve.wait_ge(s_y1, i * 2 + (t + 3))
                        dve.wait_ge(ld[t], i * 32 + 32)
                        nc.vector.tensor_tensor(y2[:, t], y1[:, t], gt[:, t], ALU.mult).then_inc(s_y2, 1)
                        dve.wait_ge(s_y2, i * 2 + (t + 1))
                        dve.wait_ge(st[t], i * 16 + 16)
                        nc.vector.scalar_tensor_tensor(y3[:, t], y2[:, t], kept["ffn_scale"][:], xt[:, t],
                                                       ALU.mult, ALU.add).then_inc(s_y3, 1)

def build(nc, X, ln_g, ln_b, Wq, bq, Wk, bk, Wv, bv, Wo, bo, w_fc, w_proj, out):
    with ExitStack() as ctx:
        def sb(name, shape, dt):
            return ctx.enter_context(nc.sbuf_tensor(name, shape, dt))
        kept = dict(
            ident32=sb("ident32", [P, P], F32), ident16=sb("ident16", [P, P], F16), identb=sb("identb", [P, P], BF16),
            mask_kq=sb("mask_kq", [P, P], BF16), mask_qk=sb("mask_qk", [P, P], BF16),
            half=sb("half", [P, JT], F32),
            scale=sb("scale", [P, 4], F32), unscale=sb("unscale", [P, 4], F32),
            amean=sb("amean", [P, 2], F32), ffn_scale=sb("ffn_scale", [P, 1], F32), out_scale=sb("out_scale", [P, 1], F32),
            qk_bias=sb("qk_bias", [P, 2, KT], F32), out_bias=sb("out_bias", [P, D], F32),
            wo_head=sb("wo_head", [P, KT, D], F16), wo_tail=sb("wo_tail", [P, KT, D], F16),
            fc_T=sb("fc_T", [P, KT, HID], F16), proj_T=sb("proj_T", [P, HT, D], F16),
        )
        qk_dram = nc.dram_tensor("qk_split", (UNITS, 2, 2, DH, S), F16, kind="Internal").ap()
        xf_dram = nc.dram_tensor("xf_split", (NT // 2, P, 2, KT, 2 * P), F16, kind="Internal").ap()
        with ExitStack() as c2:
            kept["w_head"] = c2.enter_context(nc.sbuf_tensor("w_head", [P, 3, KT, D], F16))
            kept["w_tail"] = c2.enter_context(nc.sbuf_tensor("w_tail", [P, 3, KT, D], F16))
            weights_block(nc, (ln_g, ln_b, Wq, bq, Wk, bk, Wv, bv, Wo, bo, w_fc, w_proj), kept)
            kept["v_all"] = ctx.enter_context(nc.sbuf_tensor("v_all", [P, UNITS, S // P, VW], F16, side="right"))
            project_block(nc, X, qk_dram, xf_dram, kept)
        gate_dram = nc.dram_tensor("gate", (NT, P, D), F32, kind="Internal").ap()
        attend_block(nc, qk_dram, xf_dram, gate_dram, kept)
        finish_block(nc, X, out, gate_dram, kept)


_INS = ["L0_attn_X", "L0_attn_ln_g", "L0_attn_ln_b", "L0_attn_Wq", "L0_attn_bq", "L0_attn_Wk", "L0_attn_bk", "L0_attn_Wv",
        "L0_attn_bv", "L0_attn_Wo", "L0_attn_bo", "L0_ffn_w_fc", "L0_ffn_w_proj"]


def kernel(**inputs):
    import concourse.bacc as _bacc
    from concourse.bass_utils import run_bass_kernel_spmd as _run

    nc = _bacc.Bacc("TRN2", target_bir_lowering=False, num_devices=1)
    arrays, args = {}, []
    for name in _INS:
        a = np.ascontiguousarray(inputs[name])
        arrays[f"in_{name}"] = a
        args.append(nc.dram_tensor(f"in_{name}", a.shape, mybir.dt.from_np(a.dtype), kind="ExternalInput").ap())
    out = nc.dram_tensor("out_0", (B, S, D), F32, kind="ExternalOutput").ap()
    build(nc, *args, out)
    r = _run(nc, [arrays], core_ids=[0])
    return r.results[0]["out_0"]
```

```python
from contextlib import ExitStack

import numpy as np

import concourse.bass as bass
from concourse import mybir
from concourse.alu_op_type import AluOpType as ALU

ACT = mybir.ActivationFunctionType
F32 = mybir.dt.float32
F16 = mybir.dt.float16
BF16 = mybir.dt.bfloat16
I32 = mybir.dt.int32
AX = mybir.AxisListType

P = 128
B, S, D = 2, 2048, 512
H, DH = 16, 32
HID = 1280
KT = D // P
HT = HID // P
NT = B * S // P
G = 512
JT = G // P
CH = S // G
UNITS = B * H
EPS = 1e-5
BIG = 1e30
VW = 2 * DH + 1
V_SHIFT = 2.0 ** -9
RMAX = bass.bass_isa.ReduceOp.max
Q, K, V, O = range(4)


class Steps:

    def __init__(self, eng, sem, base=0):
        self.eng, self.sem, self.base, self.n = eng, sem, base, 0

    def did(self, instruction):
        instruction.then_inc(self.sem, 1)
        self.n += 1

    def settle(self):
        self.eng.wait_ge(self.sem, self.base + self.n)


def bare(eng, sem):
    eng.sem_inc(sem)


def weights_block(nc, ins, kept):
    (ln_g, ln_b, wq, bq, wk, bk, wv, bv, wo, bo, w_fc, w_proj) = ins
    with ExitStack() as ctx:
        def sb(name, shape, dt):
            return ctx.enter_context(nc.sbuf_tensor(name, shape, dt))

        def sem(name):
            return ctx.enter_context(nc.semaphore(name))

        wf = sb("w_raw", [P, 4, KT, D], F32)
        wg = sb("w_gained", [P, 3, KT, D], F32)
        fc = sb("w_fc_raw", [P, HT, D], F32)
        pr = sb("w_proj_raw", [P, KT, HID], F32)
        fc_neg = sb("fc_neg", [P, HT, D], F16)
        pr_neg = sb("pr_neg", [P, KT, HID], F16)
        fc_t = sb("fc_ternary", [P, HT, D], F16)
        pr_t = sb("pr_ternary", [P, KT, HID], F16)
        vecs = sb("vectors", [P, 5, KT], F32)
        bo_row = sb("bo_row", [P, D], F32)
        amax = sb("amax", [P, 4], F32)
        gmax = sb("gmax", [P, 4], F32)
        pw = sb("pw", [P, 4], F32)
        rpw = sb("rpw", [P, 4], F32)
        asum = sb("asum", [P, 2], F32)
        thr = sb("thr", [P, 2], F32)
        nthr = sb("nthr", [P, 2], F32)
        am2 = sb("am2", [P, 2], F32)
        ones = sb("ones", [P, P], F32)
        vb = sb("v_bias", [P, KT], F32)
        vb_wide = sb("v_bias_wide", [P, KT, P], F32)

        tp = ctx.enter_context(nc.psum_tensor("w_tp", [P, 4, 2, 512], F16))
        pb = ctx.enter_context(nc.psum_tensor("w_bias", [P, 512], F32))
        ps = ctx.enter_context(nc.psum_tensor("w_sum", [P, 512], F32))
        po = ctx.enter_context(nc.psum_tensor("w_obias", [P, 512], F32))

        ld_w = [sem(f"ld_w{m}") for m in range(4)]
        ld_vec = sem("ld_vec")
        ld_fc, ld_pr, ld_bo = sem("ld_fc"), sem("ld_pr"), sem("ld_bo")
        s_pool = sem("s_pool")
        s_ones = sem("s_ones")
        s_gain = sem("s_gain")
        s_amax = sem("s_amax")
        s_gmax = sem("s_gmax")
        s_scale = sem("s_scale")
        s_head = sem("s_head")
        s_asum = sem("s_asum")
        s_sum = sem("s_sum")
        s_thr = sem("s_thr")
        s_tern = sem("s_tern")
        s_tp, s_tc = sem("s_tp"), sem("s_tc")
        s_bias = sem("s_bias")
        s_vbw = sem("s_vbw")
        s_obias = sem("s_obias")
        s_dve = sem("s_dve")

        with nc.Block() as block:
            @block.sync
            def _(sp):
                for m, w in enumerate((wq, wk, wv)):
                    sp.dma_start(wf[:, m], w.rearrange("(k p) n -> p k n", p=P)).then_inc(ld_w[m], 16)
                with nc.allow_non_contiguous_dma(reason="five short vectors as columns"):
                    for n, v in enumerate((ln_g, ln_b, bq, bk, bv)):
                        sp.dma_start(vecs[:, n], v.rearrange("(k p) -> p k", p=P)).then_inc(ld_vec, 16)
                sp.dma_start(fc[:], w_fc.rearrange("(k p) n -> p k n", p=P)).then_inc(ld_fc, 16)
                sp.dma_start(pr[:], w_proj.rearrange("(k p) n -> p k n", p=P)).then_inc(ld_pr, 16)
                sp.dma_start(wf[:, O], wo.rearrange("(k p) n -> p k n", p=P)).then_inc(ld_w[O], 16)
                sp.dma_start(bo_row[:], bo.rearrange("(a n) -> a n", a=1).to_broadcast([P, D])).then_inc(ld_bo, 16)

            @block.gpsimd
            def _(pool):
                own = Steps(pool, s_pool)
                own.did(nc.gpsimd.memset(ones[:], 1.0))
                for t in (kept["ident32"], kept["ident16"], kept["identb"], kept["mask_kq"], kept["mask_qk"]):
                    own.did(nc.gpsimd.memset(t[:], 0.0))
                own.did(nc.gpsimd.memset(kept["half"][:], -0.5))
                own.settle()
                for t in (kept["ident32"], kept["ident16"], kept["identb"]):
                    nc.gpsimd.affine_select(out=t[:], in_=t[:], compare_op=ALU.not_equal, fill=1.0, base=0,
                                            pattern=[[-1, P]], channel_multiplier=1).then_inc(s_ones, 1)
                nc.gpsimd.affine_select(out=kept["mask_kq"][:], in_=kept["mask_kq"][:], compare_op=ALU.is_ge, fill=-BIG,
                                        base=0, pattern=[[1, P]], channel_multiplier=-1).then_inc(s_ones, 1)
                nc.gpsimd.affine_select(out=kept["mask_qk"][:], in_=kept["mask_qk"][:], compare_op=ALU.is_ge, fill=-BIG,
                                        base=0, pattern=[[-1, P]], channel_multiplier=1).then_inc(s_ones, 1)
                for m in range(4):
                    pool.wait_ge(s_amax, m + 1)
                    nc.gpsimd.partition_all_reduce(gmax[:, m:m + 1], amax[:, m:m + 1], P, RMAX).then_inc(s_gmax, 1)

            @block.scalar
            def _(act):
                def head(m):
                    act.wait_ge(s_scale, m + 1)
                    src = wg[:, m] if m < 3 else wf[:, O]
                    nc.scalar.activation(kept["w_head"][:, m] if m < 3 else kept["wo_head"][:], src, ACT.Identity,
                                         scale=kept["scale"][:, m:m + 1]).then_inc(s_head, 1)

                for m in range(3):
                    head(m)
                for n in range(20):
                    act.wait_ge(s_tp, n + 1)
                    if n < 10:
                        dst = kept["fc_T"][:, :, n * P:(n + 1) * P]
                    else:
                        dst = kept["proj_T"][:, n - 10, :].rearrange("p (k n) -> p k n", k=KT)
                    nc.scalar.activation(dst, tp[:, n % 4, 0].rearrange("p (k n) -> p k n", k=4), ACT.Copy).then_inc(s_tc, 1)
                head(O)

            @block.vector
            def _(dve):
                own = Steps(dve, s_dve)

                def scales(m):
                    dve.wait_ge(s_gmax, m + 1)
                    c = slice(m, m + 1)
                    own.did(nc.vector.tensor_scalar(gmax[:, c], gmax[:, c], 1e-30, None, ALU.max))
                    own.settle()
                    own.did(nc.vector.tensor_single_scalar(pw[:, c].bitcast(I32), gmax[:, c].bitcast(I32), 0x7F800000, ALU.bitwise_and))
                    own.settle()
                    own.did(nc.vector.reciprocal(rpw[:, c], pw[:, c]))
                    own.settle()
                    own.did(nc.vector.tensor_scalar(kept["scale"][:, c], rpw[:, c], 2.0 ** 14, None, ALU.mult))
                    own.settle()
                    nc.vector.tensor_scalar(kept["unscale"][:, c], pw[:, c], 2.0 ** -14, None, ALU.mult).then_inc(s_scale, 1)

                def tail(m):
                    dve.wait_ge(s_head, m + 1)
                    src = wg[:, m] if m < 3 else wf[:, O]
                    hi, lo = (kept["w_head"][:, m], kept["w_tail"][:, m]) if m < 3 else (kept["wo_head"][:], kept["wo_tail"][:])
                    own.did(nc.vector.scalar_tensor_tensor(lo, src, kept["scale"][:, m:m + 1], hi, ALU.mult, ALU.subtract))

                dve.wait_ge(ld_vec, 80)
                for m in range(3):
                    dve.wait_ge(ld_w[m], 16)
                    for k in range(KT):
                        own.did(nc.vector.tensor_scalar(wg[:, m, k], wf[:, m, k], vecs[:, 0, k:k + 1], None, ALU.mult))
                    own.settle()
                    nc.vector.tensor_reduce(amax[:, m:m + 1], wg[:, m], AX.XY, ALU.max, apply_absolute_value=True).then_inc(s_amax, 1)
                    if m:
                        scales(m - 1)
                        if m > 1:
                            tail(m - 2)
                scales(2)
                tail(1)
                dve.wait_ge(ld_fc, 16)
                nc.vector.tensor_reduce(asum[:, 0:1], fc[:], AX.XY, ALU.add, apply_absolute_value=True).then_inc(s_asum, 1)
                dve.wait_ge(ld_pr, 16)
                nc.vector.tensor_reduce(asum[:, 1:2], pr[:], AX.XY, ALU.add, apply_absolute_value=True).then_inc(s_asum, 1)
                tail(2)
                dve.wait_ge(s_sum, 1)
                own.did(nc.vector.tensor_scalar(kept["amean"][:], ps[:, 0:2], 1.0 / (HID * D), 1e-5, ALU.mult, ALU.max))
                own.settle()
                own.did(nc.vector.tensor_scalar(thr[:], kept["amean"][:], 0.7, None, ALU.mult))
                own.settle()
                own.did(nc.vector.tensor_scalar(nthr[:], thr[:], -1.0, None, ALU.mult))
                own.settle()
                for raw, neg, out, c in ((fc, fc_neg, fc_t, 0), (pr, pr_neg, pr_t, 1)):
                    own.did(nc.vector.tensor_scalar(neg[:], raw[:], nthr[:, c:c + 1], None, ALU.is_lt))
                    own.settle()
                    nc.vector.scalar_tensor_tensor(out[:], raw[:], thr[:, c:c + 1], neg[:], ALU.is_gt, ALU.subtract).then_inc(s_tern, 1)
                dve.wait_ge(s_bias, 1)
                bc = pb[:, 0:12].rearrange("p (m k) -> p m k", m=3)
                nc.vector.tensor_tensor(kept["qk_bias"][:], bc[:, 0:2], vecs[:, 2:4], ALU.add).then_inc(s_dve, 1)
                own.n += 1
                own.did(nc.vector.tensor_tensor(vb[:], bc[:, 2], vecs[:, 4], ALU.add))
                own.settle()
                nc.vector.tensor_copy(vb_wide[:], vb[:].rearrange("p (k a) -> p k a", a=1).to_broadcast([P, KT, P])).then_inc(s_vbw, 1)
                dve.wait_ge(ld_w[O], 16)
                nc.vector.tensor_reduce(amax[:, O:O + 1], wf[:, O], AX.XY, ALU.max, apply_absolute_value=True).then_inc(s_amax, 1)
                scales(O)
                tail(O)
                own.did(nc.vector.tensor_tensor(am2[:, 0:1], kept["amean"][:, 0:1], kept["amean"][:, 0:1], ALU.mult))
                own.settle()
                own.did(nc.vector.tensor_tensor(am2[:, 1:2], am2[:, 0:1], kept["amean"][:, 1:2], ALU.mult))
                own.settle()
                own.did(nc.vector.tensor_scalar(kept["ffn_scale"][:], am2[:, 1:2], 8.0, None, ALU.mult))
                own.did(nc.vector.scalar_tensor_tensor(kept["out_scale"][:], kept["unscale"][:, V:V + 1], 1.0 / V_SHIFT,
                                                       kept["unscale"][:, O:O + 1], ALU.mult, ALU.mult))
                dve.wait_ge(s_obias, 1)
                dve.wait_ge(ld_bo, 16)
                own.did(nc.vector.tensor_tensor(kept["out_bias"][:], po[:], bo_row[:], ALU.add))

            @block.tensor
            def _(pe):
                pe.wait_ge(ld_vec, 80)
                for m in range(3):
                    pe.wait_ge(ld_w[m], 16)
                    for mt in range(KT):
                        for k in range(KT):
                            last = nc.tensor.matmul(pb[:, 4 * m + mt:4 * m + mt + 1], wf[:, m, k, mt * P:(mt + 1) * P],
                                                    vecs[:, 1, k:k + 1], start=(k == 0), stop=(k == KT - 1))
                last.then_inc(s_bias, 1)
                pe.wait_ge(s_asum, 2)
                pe.wait_ge(s_pool, 7)
                nc.tensor.matmul(ps[:, 0:2], ones[:], asum[:], start=True, stop=True).then_inc(s_sum, 1)
                pe.wait_ge(s_ones, 5)
                for n in range(20):
                    if n % 10 == 0:
                        pe.wait_ge(s_tern, n // 10 + 1)
                    if n >= 4:
                        pe.wait_ge(s_tc, n - 3)
                    for k in range(4):
                        src = fc_t[:, n, k * P:(k + 1) * P] if n < 10 else pr_t[:, k, (n - 10) * P:(n - 9) * P]
                        last = nc.tensor.transpose(tp[:, n % 4, 0, k * P:(k + 1) * P], src, kept["ident16"][:])
                    last.then_inc(s_tp, 1)
                pe.wait_ge(s_vbw, 1)
                pe.wait_ge(ld_w[O], 16)
                for k in range(KT):
                    last = nc.tensor.matmul(po[:], vb_wide[:, k], wf[:, O, k], start=(k == 0), stop=(k == KT - 1))
                last.then_inc(s_obias, 1)


T_PER, PJ_PER, QK_PER = 2 * JT, 3 * KT, 2 * KT
AFTER = 3
RING = 4
GROUPS = B * CH


def project_block(nc, x, qk_dram, xf_dram, kept):
    with ExitStack() as ctx:
        def sb(name, shape, dt):
            return ctx.enter_context(nc.sbuf_tensor(name, shape, dt))

        def sem(name):
            return ctx.enter_context(nc.semaphore(name))

        xin = sb("xin", [P, 2, JT, D], F32)
        xn = sb("xn", [P, JT, D], F32)
        xn2 = sb("xn2", [P, JT, D], F32)
        st6 = sb("st6", [P, JT, 6], F32)
        mv = sb("mv", [P, JT, 2], F32)
        va = sb("va", [P, JT], F32)
        r1 = sb("r1", [P, JT], F32)
        vb = sb("vb", [P, JT], F32)
        vc = sb("vc", [P, JT], F32)
        vd = sb("vd", [P, JT], F32)
        r2 = sb("r2", [P, JT], F32)
        f_head = sb("f_head", [P, 2, KT, G], F16)
        f_tail = sb("f_tail", [P, 2, KT, G], F16)
        a_head = sb("a_head", [P, 2, KT, G], F16)
        a_tail = sb("a_tail", [P, 2, KT, G], F16)
        qk32 = sb("qk32", [P, RING, G], F32)
        qk_head = sb("qk_head", [P, RING, G], F16)
        qk_tail = sb("qk_tail", [P, RING, G], F16)
        tps = ctx.enter_context(nc.psum_tensor("tps", [P, RING, 512], F32))
        pjs = ctx.enter_context(nc.psum_tensor("pjs", [P, RING, 512], F32))
        v_all = kept["v_all"]

        ld_x = [sem(f"ld_x{u}") for u in range(2)]
        s_va, s_r1, s_vd, s_r2 = sem("s_va"), sem("s_r1"), sem("s_vd"), sem("s_r2")
        s_xn, s_xn2 = sem("s_xn"), sem("s_xn2")
        s_ones = sem("s_v_ones")
        s_bare = sem("s_bare")
        s_own = sem("s_own")
        s_t = sem("s_t")
        s_th, s_tt = sem("s_th"), sem("s_tt")
        s_pj = sem("s_pj")
        s_pa = sem("s_pa")
        s_ph = sem("s_ph")
        s_pt = sem("s_pt")
        st_qk = [sem(f"st_qk{r}") for r in range(RING)]
        st_xf = [sem(f"st_xf{u}") for u in range(2)]

        OWN_PER = 2 * JT + 2

        def groups(eng, body):
            with eng.Fori(0, CH - 1) as it:
                for u in range(2):
                    body(it * 2 + u, it, u, True)
            for u in range(2):
                body(GROUPS - 2 + u, CH - 1, u, u == 0)

        def nxt(it, u):
            return (it, 1) if u == 0 else (it + 1, 0)

        with nc.Block() as block:
            @block.sync
            def _(sp):
                for r in range(RING):
                    sp.sem_inc(st_qk[r], 32)
                for u in range(2):
                    sp.sem_inc(st_xf[u], 64)

                def load_x(it, u):
                    sp.dma_start(xin[:, u], x[u, bass.ds(it * G, G), :].rearrange("(j p) d -> p j d", p=P)).then_inc(ld_x[u], 16)

                def store_xf(it, u):
                    for h in range(2):
                        for part, src in enumerate((f_head, f_tail)):
                            sp.dma_start(xf_dram[bass.ds(it * 2 + (8 * u + h), 1), :, part],
                                         src[:, u, :, 256 * h:256 * (h + 1)]).then_inc(st_xf[u], 16)

                load_x(0, 0)
                load_x(0, 1)
                sp.wait_ge(s_tt, T_PER)
                store_xf(0, 0)

                def body(g, it, u, more):
                    if more and not (isinstance(it, int) and it == CH - 1):
                        sp.wait_ge(s_xn, g * JT + JT)
                        load_x(it + 1, u)
                    for i in range(QK_PER):
                        sp.wait_ge(s_pt, g * PJ_PER + (RING + i + 1))
                        for part, src in enumerate((qk_head, qk_tail)):
                            first = 16 * u + 4 * (i % KT)
                            sp.dma_start(qk_dram[first:first + 4, i // KT, part, :, bass.ds(it * G, G)],
                                         src[:, i % RING]).then_inc(st_qk[i % RING], 16)
                    if more:
                        sp.wait_ge(s_tt, g * T_PER + 2 * T_PER)
                        store_xf(*nxt(it, u))
                groups(sp, body)
                for r in range(RING):
                    sp.wait_ge(st_qk[r], 32 + 32 * GROUPS * QK_PER // RING)
                for u in range(2):
                    sp.wait_ge(st_xf[u], 64 + 64 * CH)

            @block.gpsimd
            def _(pool):
                def norms(g):
                    pool.wait_ge(s_va, g + 1)
                    nc.gpsimd.tensor_tensor(r1[:], va[:], kept["half"][:], ALU.pow).then_inc(s_r1, 1)
                    pool.wait_ge(s_vd, g + 1)
                    nc.gpsimd.tensor_tensor(r2[:], vd[:], kept["half"][:], ALU.pow).then_inc(s_r2, 1)

                def second(g, first):
                    pool.wait_ge(s_r2, g + 1)
                    for j in range(JT):
                        pool.wait_ge(s_xn, g * JT + (j + 1))
                        if not first:
                            pool.wait_ge(s_t, g * T_PER + (2 * j + 2 - T_PER))
                        bare(pool, s_bare)
                        nc.gpsimd.tensor_scalar(xn2[:, j], xn[:, j], r2[:, j:j + 1], 1.0, ALU.mult, ALU.mult).then_inc(s_xn2, 1)

                norms(0)
                second(0, True)
                nc.gpsimd.memset(v_all[:, :, :, 2 * DH:VW], 1.0).then_inc(s_ones, 1)

                def body(g, it, u, more):
                    if more:
                        norms(g + 1)
                        second(g + 1, False)
                    for i in range(QK_PER):
                        pool.wait_ge(s_pa, g * PJ_PER + (RING + i + 1))
                        pool.wait_ge(st_qk[i % RING], g * (32 * QK_PER // RING) + (32 * (i // RING) + 32))
                        bare(pool, s_bare)
                        nc.gpsimd.tensor_scalar(qk_head[:, i % RING], qk32[:, i % RING], 1.0, 0.0, ALU.mult, ALU.add).then_inc(s_ph, 1)
                groups(pool, body)

            @block.scalar
            def _(act):
                act.sem_inc(s_pa, RING)

                def head(g, i, it, u):
                    act.wait_ge(s_t, g * T_PER + (i + 1))
                    if i == 0:
                        act.wait_ge(st_xf[u], it * 64 + 64)
                    dst = f_head if i % 2 == 0 else a_head
                    nc.scalar.activation(dst[:, u, :, P * (i // 2):P * (i // 2 + 1)],
                                         tps[:, i % RING].rearrange("p (k n) -> p k n", k=KT), ACT.Copy).then_inc(s_th, 1)

                for i in range(T_PER):
                    head(0, i, 0, 0)

                def body(g, it, u, more):
                    for i in range(PJ_PER):
                        act.wait_ge(s_pj, g * PJ_PER + (i + 1))
                        if i < QK_PER:
                            act.wait_ge(s_pt, g * PJ_PER + (i + 1))
                            m, mt = divmod(i, KT)
                            nc.scalar.activation(qk32[:, i % RING], pjs[:, i % RING], ACT.Identity,
                                                 scale=kept["unscale"][:, m:m + 1],
                                                 bias=kept["qk_bias"][:, m, mt:mt + 1]).then_inc(s_pa, 1)
                        else:
                            nc.scalar.activation(v_all[:, H * u:H * (u + 1), bass.ds(it * JT + (i - QK_PER), 1), DH:2 * DH],
                                                 pjs[:, i % RING].rearrange("p (h a d) -> p h a d", a=1, h=H), ACT.Copy,
                                                 scale=V_SHIFT).then_inc(s_pa, 1)
                        if more and 0 <= i - AFTER < T_PER:
                            head(g + 1, i - AFTER, *nxt(it, u))
                groups(act, body)

            @block.vector
            def _(dve):
                dve.sem_inc(s_pt, RING)

                def norms(g, it, u, first):
                    own = Steps(dve, s_own, g * OWN_PER)
                    dve.wait_ge(ld_x[u], it * 16 + 16)
                    for j in range(JT):
                        own.did(nc.vector.bn_stats(st6[:, j], xin[:, u, j]))
                    own.settle()
                    bare(dve, s_bare)
                    for j in range(JT):
                        own.did(nc.vector.bn_aggr(mv[:, j], st6[:, j]))
                    own.settle()
                    nc.vector.tensor_scalar(va[:], mv[:, :, 1], EPS, None, ALU.add).then_inc(s_va, 1)
                    dve.wait_ge(s_r1, g + 1)
                    for j in range(JT):
                        if not first:
                            dve.wait_ge(s_t, g * T_PER + (2 * j + 1 - T_PER))
                            dve.wait_ge(s_xn2, g * JT + (j + 1 - JT))
                        nc.vector.tensor_scalar(xn[:, j], xin[:, u, j], mv[:, j, 0:1], r1[:, j:j + 1],
                                                ALU.subtract, ALU.mult).then_inc(s_xn, 1)
                        if j == 0:
                            own.did(nc.vector.tensor_tensor(vb[:], mv[:, :, 1], r1[:], ALU.mult))
                            own.settle()
                            own.did(nc.vector.tensor_tensor(vc[:], vb[:], r1[:], ALU.mult))
                            own.settle()
                            nc.vector.tensor_scalar(vd[:], vc[:], EPS, None, ALU.add).then_inc(s_vd, 1)
                    assert own.n == OWN_PER

                def tail(g, i, u):
                    dve.wait_ge(s_th, g * T_PER + (i + 1))
                    hi, lo = (f_head, f_tail) if i % 2 == 0 else (a_head, a_tail)
                    c = slice(P * (i // 2), P * (i // 2 + 1))
                    nc.vector.tensor_tensor(lo[:, u, :, c], tps[:, i % RING].rearrange("p (k n) -> p k n", k=KT),
                                            hi[:, u, :, c], ALU.subtract).then_inc(s_tt, 1)

                norms(0, 0, 0, True)
                for i in range(T_PER):
                    tail(0, i, 0)

                def body(g, it, u, more):
                    if more:
                        norms(g + 1, *nxt(it, u), False)
                    for i in range(PJ_PER):
                        if i < QK_PER:
                            dve.wait_ge(s_ph, g * QK_PER + (i + 1))
                            nc.vector.tensor_tensor(qk_tail[:, i % RING], qk32[:, i % RING], qk_head[:, i % RING],
                                                    ALU.subtract).then_inc(s_pt, 1)
                        else:
                            dve.wait_ge(s_pa, g * PJ_PER + (RING + i + 1))
                            vt = v_all[:, H * u:H * (u + 1), bass.ds(it * JT + (i - QK_PER), 1), :].rearrange("p h a d -> p (h a) d")
                            nc.vector.scalar_tensor_tensor(vt[:, :, 0:DH], pjs[:, i % RING].rearrange("p (h d) -> p h d", h=H),
                                                           V_SHIFT, vt[:, :, DH:2 * DH], ALU.mult, ALU.subtract).then_inc(s_pt, 1)
                        if more and 0 <= i - AFTER < T_PER:
                            tail(g + 1, i - AFTER, nxt(it, u)[1])
                groups(dve, body)

            @block.tensor
            def _(pe):
                def transpose(g, i, first):
                    j = i // 2
                    pe.wait_ge(s_xn if i % 2 == 0 else s_xn2, g * JT + (j + 1))
                    if not (first and i < RING):
                        pe.wait_ge(s_tt, g * T_PER + (i + 1 - RING))
                    src = xn if i % 2 == 0 else xn2
                    for k in range(KT):
                        last = nc.tensor.transpose(tps[:, i % RING, k * P:(k + 1) * P], src[:, j, k * P:(k + 1) * P],
                                                   kept["ident32"][:])
                    last.then_inc(s_t, 1)

                for i in range(T_PER):
                    transpose(0, i, True)

                wh, wt = kept["w_head"], kept["w_tail"]

                def body(g, it, u, more):
                    pe.wait_ge(s_tt, g * T_PER + T_PER)
                    for i in range(PJ_PER):
                        pe.wait_ge(s_pa, g * PJ_PER + (i + 1))
                        pe.wait_ge(s_pt, g * PJ_PER + (i + 1))
                        m, mt = divmod(i, KT)
                        for k in range(KT):
                            ws = slice(mt * P, (mt + 1) * P)
                            if m < V:
                                pairs = [(wh[:, m, k, ws], a_head[:, u, k]), (wh[:, m, k, ws], a_tail[:, u, k]),
                                         (wt[:, m, k, ws], a_head[:, u, k])]
                            else:
                                pairs = [(a_head[:, u, k, ws], wh[:, m, k]), (a_head[:, u, k, ws], wt[:, m, k]),
                                         (a_tail[:, u, k, ws], wh[:, m, k])]
                            for n, (a, b) in enumerate(pairs):
                                last = nc.tensor.matmul(pjs[:, i % RING], a, b, start=(k == 0 and n == 0),
                                                        stop=(k == KT - 1 and n == 2))
                        last.then_inc(s_pj, 1)
                        if more and 0 <= i - AFTER < T_PER:
                            transpose(g + 1, i - AFTER, False)
                groups(pe, body)


QB = S // P
NG = S // G
LAG = 5
TAIL_LAG = LAG - 2
HD_RING, TL_RING, W_RING = 8, 5, 5
SHIFT = HD_RING
AV_CREDIT = 4
MX_LEAD = 28
POOL_SHARE = (0.45, 0.6)
P_SHIFT = 10
SCALE = DH ** -0.5
FT = 2 * P


def attention_steps():
    steps = []
    for g in range(NG):
        for j in range(0, JT * (g + 1), 2):
            parts, at = [], 0
            for key in (j, j + 1):
                q0 = max(0, key - JT * g) * P
                parts.append((key, q0, at))
                at += G - q0
            steps.append((g, parts, at))
    return steps


def maximum_rounds():
    return [(i, c, min(G, (i + 1) * P - c * G)) for i in range(QB) for c in range(i // JT + 1)]


STEPS, ROUNDS = attention_steps(), maximum_rounds()
NS = len(STEPS)
NR = len(ROUNDS)
assert NR == 2 * NS
POOL_COLS = [[int(cols * share) // 32 * 32 for _, _, cols in STEPS] for share in POOL_SHARE]
F1_AT = {1 + 2 * m: m for m in range(HT)}
F2_AT = {22 + c: (0, c) for c in range(5)} | {30 + c: (1, c) for c in range(5)}


def attend_block(nc, qk_dram, xf_dram, gate_dram, kept):
    with ExitStack() as ctx:
        def sb(name, shape, dt):
            return ctx.enter_context(nc.sbuf_tensor(name, shape, dt))

        def sem(name):
            return ctx.enter_context(nc.semaphore(name))

        q_mx = [sb(f"q_mx{u}", [P, S], F16) for u in range(2)]
        k_mx = [sb(f"k_mx{u}", [P, S], F16) for u in range(2)]
        q_st = [sb(f"q_st{u}", [P, S], F16) for u in range(2)]
        k_st = [sb(f"k_st{u}", [P, S], F16) for u in range(2)]
        w32 = sb("w32", [P, W_RING, 2 * G], F32)
        w_hd = sb("w_hd", [P, HD_RING, 2 * G], F16)
        w_tl = sb("w_tl", [P, TL_RING, 2 * G], F16)
        v_st = sb("v_st", [P, 2, QB, VW], F16)
        mx = sb("mx", [P, NG, QB], F32)
        mm = sb("mm", [P, QB], F32)
        mneg = sb("mneg", [P, QB], F32)
        m_ht = sb("m_ht", [P, 2, QB], F16)
        m_rows = sb("m_rows", [2 * QB, P], F16)
        o_raw = sb("o_raw", [P, 2, QB, VW], F32)
        rden = sb("rden", [P, QB], F32)
        xf = sb("xf", [P, 2, KT, FT], F16)
        r32 = sb("r32", [P, 2, FT], F32)
        s_hd = sb("s_hd", [P, HT, FT], F16)
        s_tl = sb("s_tl", [P, HT, FT], F16)
        g32 = sb("g32", [P, 2, D], F32)
        st_ps = ctx.enter_context(nc.psum_tensor("st_ps", [P, 2, 2 * G], F32))
        mx_ps = ctx.enter_context(nc.psum_tensor("mx_ps", [P, 2, G], F32))
        av_ps = ctx.enter_context(nc.psum_tensor("av_ps", [P, G], F32))
        ff_ps = ctx.enter_context(nc.psum_tensor("ff_ps", [P, D], F32))
        av = av_ps[:, 0:JT * VW].rearrange("p (i v) -> p i v", i=JT)
        v_all = kept["v_all"]

        ld_mx = [sem(f"ld_mx{u}") for u in range(2)]
        ld_st = [sem(f"ld_st{u}") for u in range(2)]
        ld_mr = [sem(f"ld_mr{u}") for u in range(2)]
        ld_xf = sem("ld_xf")
        st_g = [sem(f"st_g{u}") for u in range(2)]
        s_set = sem("s_set")
        s_st = sem("s_st")
        s_exp = sem("s_exp")
        s_head = sem("s_head_a")
        s_tld = sem("s_tld")
        s_tlp = sem("s_tlp")
        s_av = sem("s_av")
        s_avc = sem("s_avc")
        s_vs = sem("s_vs")
        s_mx = sem("s_mx")
        s_mr = sem("s_mr")
        s_m = sem("s_m")
        s_mh = sem("s_mh")
        s_tm = sem("s_tm")
        s_row = sem("s_row")
        s_rd = sem("s_rd")
        s_os = sem("s_os")
        s_on = sem("s_on")
        s_oh = sem("s_oh")
        s_ot = sem("s_ot")
        s_f1 = sem("s_f1")
        s_re = sem("s_re")
        s_sq = sem("s_sq")
        s_sh = sem("s_sh")
        s_sl = sem("s_sl")
        s_f2 = sem("s_f2")
        s_e = sem("s_e")
        s_ga = sem("s_ga")
        s_bare = sem("s_bare_a")

        PAIRS = UNITS // 2
        N2 = 2 * NS

        def place(it, n):
            return it * 2 + n // NS, (n // NS) % 2, it + n // N2, n % NS

        def split_done(eng, count):
            eng.wait_ge(s_tlp, count)
            eng.wait_ge(s_tld, count)

        def exists(it, n):
            return not (isinstance(it, int) and it * N2 + n >= UNITS * NS)

        def before(it, n, k):
            return isinstance(it, int) and it * N2 + n < k

        def pairs(eng, body):
            with eng.Fori(0, PAIRS - 1) as it:
                body(it)
            body(PAIRS - 1)

        def all_steps(eng, step):
            for n in range(SHIFT):
                step(0, n)
            with eng.Fori(0, PAIRS - 1) as it:
                for n in range(SHIFT, SHIFT + N2):
                    step(it, n)
            for n in range(SHIFT, N2):
                step(PAIRS - 1, n)

        with nc.Block() as block:
            @block.sync
            def _(sp):
                for u in range(2):
                    sp.sem_inc(st_g[u], 16)

                def load_operands(unit, q_to, k_to, semaphore):
                    src = qk_dram[bass.ds(unit, 1)]
                    hd_tl = lambda m: src[:, m].rearrange("a t d s -> (a t d) s")
                    hd = lambda m: src[:, m, 0].rearrange("a d s -> (a d) s")
                    sp.dma_start(q_to[0:64, :], hd_tl(0)).then_inc(semaphore, 16)
                    sp.dma_start(q_to[64:96, :], hd(0)).then_inc(semaphore, 16)
                    sp.dma_start(k_to[0:32, :], hd(1)).then_inc(semaphore, 16)
                    sp.dma_start(k_to[32:96, :], hd_tl(1)).then_inc(semaphore, 16)

                def store_rows(unit, u):
                    sp.wait_ge(s_row, unit + 1)
                    for t in range(2):
                        sp.dma_start(q_st[u][96 + t:97 + t, :].rearrange("a (i c) -> a i c", i=QB),
                                     m_rows[QB * t:QB * (t + 1), :]).then_inc(ld_mr[u], 16)

                load_operands(0, q_mx[0], k_mx[0], ld_mx[0])
                load_operands(1, q_mx[1], k_mx[1], ld_mx[1])
                load_operands(0, q_st[0], k_st[0], ld_st[0])
                sp.dma_start(xf[:], xf_dram[0]).then_inc(ld_xf, 16)
                store_rows(0, 0)

                def store_gates(it):
                    for t in range(2):
                        sp.wait_ge(s_ga, it * 2 + (t + 2))
                        sp.dma_start(gate_dram[bass.ds(it * 2 + t, 1)].rearrange("a p d -> (a p) d"), g32[:, t]).then_inc(st_g[t], 16)

                def body(it):
                    last = isinstance(it, int)
                    for u in range(2):
                        unit = it * 2 + u
                        if not last:
                            load_operands(unit + 2, q_mx[u], k_mx[u], ld_mx[u])
                        if not (last and u == 1):
                            sp.wait_ge(s_st, unit * NS + 1)
                            load_operands(unit + 1, q_st[1 - u], k_st[1 - u], ld_st[1 - u])
                            store_rows(unit + 1, 1 - u)
                        if not last and u == 0:
                            sp.wait_ge(s_f1, it * HT + HT)
                            sp.dma_start(xf[:], xf_dram[bass.ds(it + 1, 1)].rearrange("a p t k n -> (a p) t k n")).then_inc(ld_xf, 16)
                    store_gates(it)
                pairs(sp, body)
                for t in range(2):
                    sp.wait_ge(st_g[t], 16 + 16 * PAIRS)

            @block.tensor
            def _(pe):
                pe.sem_inc(s_st, 1)
                pe.sem_inc(s_av, AV_CREDIT)
                pe.sem_inc(s_f2, 1)

                def scores(it, n):
                    unit, u, nth_pair, s = place(it, n)
                    g, parts, _ = STEPS[s]
                    if s == 0:
                        pe.wait_ge(ld_st[u], nth_pair * 64 + 64)
                        pe.wait_ge(ld_mr[u], nth_pair * 32 + 32)
                    if not before(it, n, 2):
                        pe.wait_ge(s_exp, unit * NS + (s - 1))
                    for key, q0, at in parts:
                        out = st_ps[:, n % 2, at:at + G - q0]
                        kt = k_st[u][0:98, key * P:(key + 1) * P]
                        diagonal = key >= JT * g
                        last = nc.tensor.matmul(out, kt, q_st[u][0:98, g * G + q0:(g + 1) * G], start=True, stop=not diagonal)
                        if diagonal:
                            last = nc.tensor.matmul(out[:, 0:P], kept["identb"][:], kept["mask_kq"][:], start=False, stop=True)
                    last.then_inc(s_st, 1)

                def maxima(unit, u, nth_pair, r):
                    if r == 0:
                        pe.wait_ge(ld_mx[u], nth_pair * 64 + 64)
                    if not (isinstance(unit, int) and unit == 0 and r < 2):
                        pe.wait_ge(s_mr, unit * NR + r)
                    if r == 2 and not (isinstance(unit, int) and unit == 0):
                        pe.wait_ge(s_row, unit)
                    i, c, w = ROUNDS[r]
                    diagonal = c == i // JT
                    out = mx_ps[:, r % 2, 0:w]
                    last = nc.tensor.matmul(out, q_mx[u][0:96, i * P:(i + 1) * P], k_mx[u][0:96, c * G:c * G + w],
                                            start=True, stop=not diagonal)
                    if diagonal:
                        last = nc.tensor.matmul(out[:, w - P:w], kept["identb"][:], kept["mask_qk"][:], start=False, stop=True)
                    last.then_inc(s_mx, 1)

                def transpose_maxima(unit, follows):
                    pe.wait_ge(s_mh, unit + 1)
                    pe.wait_ge(s_mr, unit * NR + (NR + follows))
                    nc.tensor.transpose(mx_ps[0:2 * QB, 0, 0:P // 2].bitcast(F16), m_ht[:].rearrange("p t i -> p (t i)"),
                                        kept["ident16"][:]).then_inc(s_tm, 1)

                def weighted(it, n):
                    unit, u, _, s = place(it, n)
                    g, parts, _ = STEPS[s]
                    if s == 0:
                        pe.wait_ge(s_vs, unit + 1)
                    if parts[0][0] == 0:
                        pe.wait_ge(s_avc, unit * NG + (g + 1))
                    split_done(pe, unit * NS + (s + 1))
                    for key, q0, at in parts:
                        for w, slot, v0 in ((w_hd, n % HD_RING, 0), (w_tl, n % TL_RING, DH)):
                            for i in range(q0 // P, JT):
                                c = at + i * P - q0
                                last = nc.tensor.matmul(av[:, i, v0:VW], w[:, slot, c:c + P], v_st[:, u, key, v0:VW],
                                                        start=(key == 0 and w is w_hd and i == 0),
                                                        stop=(key == JT * g + JT - 1 and w is w_tl and i == JT - 1),
                                                        skip_group_check=True)
                    last.then_inc(s_av, 1)

                def hidden(it, m):
                    if m == 0:
                        pe.wait_ge(ld_xf, it * 16 + 16)
                        pe.wait_ge(s_ga, it * 2 + 1)
                    else:
                        pe.wait_ge(s_re, it * HT + m)
                    for k in range(KT):
                        for t in range(2):
                            last = nc.tensor.matmul(ff_ps[:, 0:FT], kept["fc_T"][:, k, m * P:(m + 1) * P], xf[:, t, k],
                                                    start=(k == 0 and t == 0), stop=(k == KT - 1 and t == 1))
                    last.then_inc(s_f1, 1)

                def outward(it, t, c):
                    if t == 0:
                        if c == 0:
                            pe.wait_ge(s_re, it * HT + HT)
                        pe.wait_ge(s_sl, it * HT + (2 * c + 4))
                    elif c == 0:
                        pe.wait_ge(s_ga, it * 2 + 2)
                    for m in (2 * c, 2 * c + 1):
                        for w in (s_hd, s_tl):
                            last = nc.tensor.matmul(ff_ps[:], w[:, m, t * P:(t + 1) * P], kept["proj_T"][:, m],
                                                    start=(m == 0 and w is s_hd), stop=(m == HT - 1 and w is s_tl))
                    if c == 4:
                        last.then_inc(s_f2, 1)

                for r in range(NR):
                    maxima(0, 0, 0, r)
                maxima(1, 1, 0, 0)
                maxima(1, 1, 0, 1)
                transpose_maxima(0, 2)
                pe.wait_ge(s_set, NG + 1)
                for n in range(1, MX_LEAD - NS):
                    maxima(1, 1, 0, 2 * n)
                    maxima(1, 1, 0, 2 * n + 1)
                    if n <= LAG:
                        scores(0, n - 1)

                def step(it, n):
                    pair, m = it + n // N2, n % N2
                    if exists(it, n + LAG):
                        scores(it, n + LAG)
                    ahead = exists(it, n + MX_LEAD)
                    unit, u, nth_pair, s = place(it, n + MX_LEAD)
                    if ahead:
                        maxima(unit, u, nth_pair, 2 * s)
                    weighted(it, n)
                    if ahead:
                        maxima(unit, u, nth_pair, 2 * s + 1)
                    if m in F1_AT:
                        hidden(pair, F1_AT[m])
                    if m in F2_AT:
                        outward(pair, *F2_AT[m])
                    if s == 0 and exists(it, n + MX_LEAD - 1):
                        transpose_maxima(unit - 1, 2 if ahead else 0)
                all_steps(pe, step)

            @block.scalar
            def _(act):
                act.sem_inc(s_avc, 1)

                def weights(it, n, between=None):
                    unit, u, _, s = place(it, n)
                    cols = STEPS[s][2]
                    scores = st_ps[:, n % 2, 0:cols]
                    act.wait_ge(s_st, unit * NS + (s + 2))
                    if not before(it, n, HD_RING):
                        act.wait_ge(s_av, unit * NS + (s + AV_CREDIT + 1 - HD_RING))
                    nc.scalar.activation(w_hd[:, n % HD_RING, 0:cols], scores, ACT.Exp, scale=SCALE).then_inc(s_head, 1)
                    if between:
                        between()
                    if not before(it, n, W_RING):
                        split_done(act, unit * NS + (s + 1 - W_RING))
                    nc.scalar.activation(w32[:, n % W_RING, 0:cols], scores, ACT.Exp, scale=SCALE).then_inc(s_exp, 1)

                def copy_out(it, n):
                    unit, u, _, s = place(it, n)
                    g = STEPS[s][0]
                    act.wait_ge(s_av, unit * NS + (s + AV_CREDIT + 1))
                    if g == 0:
                        act.wait_ge(s_ot, unit + 1)
                    nc.scalar.activation(o_raw[:, u, JT * g:JT * (g + 1)], av, ACT.Copy).then_inc(s_avc, 1)

                def relu(it, m):
                    act.wait_ge(s_f1, it * HT + (m + 1))
                    act.wait_ge(s_sl, it * HT + (m + 1))
                    nc.scalar.activation(r32[:, m % 2], ff_ps[:, 0:FT], ACT.Relu, scale=0.25).then_inc(s_re, 1)

                def gate_tanh(it, t):
                    act.wait_ge(s_f2, it * 2 + (t + 2))
                    act.wait_ge(st_g[t], it * 16 + 16)
                    nc.scalar.activation(g32[:, t], ff_ps[:], ACT.Tanh, scale=kept["ffn_scale"][:]).then_inc(s_e, 1)

                for n in range(LAG):
                    weights(0, n)

                def step(it, n):
                    pair, m, s = it + n // N2, n % N2, n % NS
                    ends = s == NS - 1 or STEPS[s + 1][0] != STEPS[s][0]
                    if exists(it, n + LAG):
                        weights(it, n + LAG, (lambda: copy_out(it, n)) if ends else None)
                    elif ends:
                        copy_out(it, n)
                    if m in F1_AT:
                        relu(pair, F1_AT[m])
                    if m in F2_AT and F2_AT[m][1] == 4:
                        gate_tanh(pair, F2_AT[m][0])
                all_steps(act, step)

            @block.gpsimd
            def _(pool):
                pool.sem_inc(s_sl, 2)

                def tail(it, n):
                    unit, u, _, s = place(it, n)
                    c = slice(0, POOL_COLS[u][s])
                    pool.wait_ge(s_exp, unit * NS + (s + 1))
                    pool.wait_ge(s_head, unit * NS + (s + 1))
                    if not before(it, n, TL_RING):
                        pool.wait_ge(s_av, unit * NS + (s + AV_CREDIT + 1 - TL_RING))
                    nc.gpsimd.tensor_tensor(w_tl[:, n % TL_RING, c], w32[:, n % W_RING, c], w_hd[:, n % HD_RING, c],
                                            ALU.subtract).then_inc(s_tlp, 1)

                def square(it, m):
                    pool.wait_ge(s_re, it * HT + (m + 1))
                    if m == 0:
                        pool.wait_ge(s_f2, it * 2 + 1)
                    nc.gpsimd.tensor_tensor(r32[:, m % 2], r32[:, m % 2], r32[:, m % 2], ALU.mult).then_inc(s_sq, 1)
                    pool.wait_ge(s_sq, it * HT + (m + 1))
                    bare(pool, s_bare)
                    nc.gpsimd.tensor_scalar(s_hd[:, m], r32[:, m % 2], 1.0, 0.0, ALU.mult, ALU.add).then_inc(s_sh, 1)
                    pool.wait_ge(s_sh, it * HT + (m + 1))
                    nc.gpsimd.tensor_tensor(s_tl[:, m], r32[:, m % 2], s_hd[:, m], ALU.subtract).then_inc(s_sl, 1)

                def normalise(unit, u):
                    pool.wait_ge(s_rd, unit + 1)
                    o = o_raw[:, u, :, 0:DH]
                    nc.gpsimd.tensor_tensor(o, o, o_raw[:, u, :, DH:2 * DH], ALU.add).then_inc(s_os, 1)
                    pool.wait_ge(s_os, unit + 1)
                    nc.gpsimd.tensor_tensor(o, o, rden[:].rearrange("p (i a) -> p i a", a=1).to_broadcast([P, QB, DH]),
                                            ALU.mult).then_inc(s_on, 1)

                for n in range(TAIL_LAG):
                    tail(0, n)

                def step(it, n):
                    pair, m, s = it + n // N2, n % N2, n % NS
                    if exists(it, n + TAIL_LAG):
                        tail(it, n + TAIL_LAG)
                    if m in F1_AT:
                        square(pair, F1_AT[m])
                    if s == 2 and not before(it, n, NS):
                        unit, u, _, _ = place(it, n)
                        normalise(unit - 1, 1 - u)
                all_steps(pool, step)
                normalise(UNITS - 1, 1)

            @block.vector
            def _(dve):
                dve.sem_inc(s_mr, 1)
                dve.sem_inc(s_ot, 2)
                dve.sem_inc(s_ga, 1)
                for c in range(1, NG):
                    nc.vector.memset(mx[:, c, 0:JT * c], -BIG).then_inc(s_set, 1)
                for k in k_st:
                    nc.vector.memset(k[96:98, :], 256.0).then_inc(s_set, 1)
                dve.wait_ge(s_set, NG + 1)

                def reduce(unit, r):
                    dve.wait_ge(s_mx, unit * NR + (r + 1))
                    i, c, w = ROUNDS[r]
                    nc.vector.tensor_reduce(mx[:, c, i:i + 1], mx_ps[:, r % 2, 0:w], AX.X, ALU.max).then_inc(s_mr, 1)

                def split_maxima(unit):
                    dve.wait_ge(s_mr, unit * NR + (NR + 1))
                    nc.vector.tensor_reduce(mm[:], mx[:].rearrange("p c i -> p i c"), AX.X, ALU.max).then_inc(s_m, 1)
                    dve.wait_ge(s_m, unit * 3 + 1)
                    nc.vector.tensor_scalar(mneg[:], mm[:], -1.0 / 256, float(P_SHIFT * np.log(2.0) / SCALE / 256),
                                            ALU.mult, ALU.add).then_inc(s_m, 1)
                    dve.wait_ge(s_m, unit * 3 + 2)
                    nc.vector.tensor_copy(m_ht[:, 0], mneg[:]).then_inc(s_m, 1)
                    dve.wait_ge(s_m, unit * 3 + 3)
                    nc.vector.tensor_tensor(m_ht[:, 1], mneg[:], m_ht[:, 0], ALU.subtract).then_inc(s_mh, 1)

                def copy_rows(unit, u, nth_pair):
                    dve.wait_ge(s_tm, unit + 1)
                    if not (isinstance(unit, int) and unit == 0):
                        v, p = (1 - u), (nth_pair if u == 1 else nth_pair - 1)
                        dve.wait_ge(ld_mr[v], p * 32 + 32)
                    nc.vector.tensor_copy(m_rows[:], mx_ps[0:2 * QB, 0, 0:P // 2].bitcast(F16)).then_inc(s_row, 1)

                def place_v(unit, u):
                    bare(dve, s_bare)
                    nc.vector.tensor_copy(v_st[:, u], v_all[:, bass.ds(unit, 1)].rearrange("p a i v -> p (a i) v")).then_inc(s_vs, 1)

                def tail(it, n):
                    unit, u, _, s = place(it, n)
                    c = slice(POOL_COLS[u][s], STEPS[s][2])
                    dve.wait_ge(s_exp, unit * NS + (s + 1))
                    dve.wait_ge(s_head, unit * NS + (s + 1))
                    if not before(it, n, TL_RING):
                        dve.wait_ge(s_av, unit * NS + (s + AV_CREDIT + 1 - TL_RING))
                    nc.vector.tensor_tensor(w_tl[:, n % TL_RING, c], w32[:, n % W_RING, c], w_hd[:, n % HD_RING, c],
                                            ALU.subtract).then_inc(s_tld, 1)

                def reciprocals(unit, u):
                    dve.wait_ge(s_avc, unit * NG + (NG + 1))
                    nc.vector.reciprocal(rden[:], o_raw[:, u, :, 2 * DH]).then_inc(s_rd, 1)

                def split_output(unit, u):
                    dve.wait_ge(s_on, unit + 1)
                    at = v_all[:, bass.ds(unit, 1)].rearrange("p a i v -> p (a i) v")
                    o = o_raw[:, u, :, 0:DH]
                    bare(dve, s_bare)
                    nc.vector.tensor_copy(at[:, :, 0:DH], o).then_inc(s_oh, 1)
                    dve.wait_ge(s_oh, unit + 1)
                    nc.vector.tensor_tensor(at[:, :, DH:2 * DH], o, at[:, :, 0:DH], ALU.subtract).then_inc(s_ot, 1)

                def gate(it, t):
                    dve.wait_ge(s_e, it * 2 + (t + 1))
                    nc.vector.scalar_tensor_tensor(g32[:, t], g32[:, t], 1.0, ff_ps[:], ALU.add, ALU.mult).then_inc(s_ga, 1)

                for r in range(NR):
                    reduce(0, r)
                split_maxima(0)
                reduce(1, 0)
                reduce(1, 1)
                copy_rows(0, 0, 0)
                place_v(0, 0)
                for n in range(1, MX_LEAD - NS):
                    reduce(1, 2 * n)
                    reduce(1, 2 * n + 1)
                    if n <= TAIL_LAG:
                        tail(0, n - 1)

                def step(it, n):
                    pair, m, s = it + n // N2, n % N2, n % NS
                    unit, u, _, _ = place(it, n)
                    ahead = exists(it, n + MX_LEAD)
                    mx_unit, _, _, mx_s = place(it, n + MX_LEAD)
                    if ahead:
                        reduce(mx_unit, 2 * mx_s)
                    if exists(it, n + TAIL_LAG):
                        tail(it, n + TAIL_LAG)
                    if ahead:
                        reduce(mx_unit, 2 * mx_s + 1)
                        if mx_s == NS - 1:
                            split_maxima(mx_unit)
                    if mx_s == 0 and exists(it, n + MX_LEAD - 1):
                        copy_rows(*place(it, n + MX_LEAD - 1)[:3])
                    if s == 10 and exists(it, n + NS):
                        dve.wait_ge(s_av, unit * NS + AV_CREDIT)
                        place_v(unit + 1, 1 - u)
                    if m in F2_AT and F2_AT[m][1] == 4:
                        gate(pair, F2_AT[m][0])
                    if not before(it, n, NS):
                        if s == 1:
                            reciprocals(unit - 1, 1 - u)
                        if s == 4:
                            split_output(unit - 1, 1 - u)
                all_steps(dve, step)
                reciprocals(UNITS - 1, 1)
                split_output(UNITS - 1, 1)


def finish_block(nc, x, out, gate_dram, kept):
    RX = 4
    with ExitStack() as ctx:
        def sb(name, shape, dt):
            return ctx.enter_context(nc.sbuf_tensor(name, shape, dt))

        def sem(name):
            return ctx.enter_context(nc.semaphore(name))

        xt = sb("xt", [P, RX, D], F32)
        gt = sb("gt", [P, RX, D], F32)
        og = sb("og", [P, 2, 2, D], F16)
        oT = sb("oT", [P, 2, 2, KT, P], F16)
        y1 = sb("y1", [P, 2, D], F32)
        y2 = sb("y2", [P, 2, D], F32)
        y3 = sb("y3", [P, RX, D], F32)
        tps = ctx.enter_context(nc.psum_tensor("o_tp", [P, 2, 2, D], F16))
        pso = ctx.enter_context(nc.psum_tensor("o_pj", [P, 2, D], F32))
        v_all = kept["v_all"]

        ld = [sem(f"ld_t{r}") for r in range(RX)]
        st = [sem(f"st_t{r}") for r in range(RX)]
        s_bare = sem("s_bare_f")
        s_g = sem("s_og")
        s_t, s_c = sem("s_ot_t"), sem("s_ot_c")
        s_p = sem("s_op")
        s_y1 = sem("s_y1")
        s_y2 = sem("s_y2")
        s_y3 = sem("s_y3")
        TURNS = QB // 2

        def turns(eng, body):
            with eng.Fori(0, TURNS - 1) as j:
                for r in range(RX):
                    body(j, r, True)
            for r in range(RX):
                body(TURNS - 1, r, r < 2)

        with nc.Block() as block:
            @block.sync
            def _(sp):
                for r in range(RX):
                    sp.sem_inc(st[r], 16)

                def load(j, r):
                    sp.dma_start(xt[:, r], x[r % 2, bass.ds(j * (2 * P) + r // 2 * P, P), :]).then_inc(ld[r], 16)
                    sp.dma_start(gt[:, r], gate_dram[bass.ds(j * 2 + (QB * (r % 2) + r // 2), 1)]
                                 .rearrange("a p d -> (a p) d")).then_inc(ld[r], 16)

                for r in range(RX):
                    load(0, r)

                def body(j, r, ahead):
                    sp.wait_ge(s_y3, j * RX + (r + 3))
                    sp.dma_start(out[r % 2, bass.ds(j * (2 * P) + r // 2 * P, P), :], y3[:, r]).then_inc(st[r], 16)
                    if not isinstance(j, int):
                        load(j + 1, r)
                turns(sp, body)
                for r in range(RX):
                    sp.wait_ge(st[r], 16 + 16 * TURNS)

            @block.tensor
            def _(pe):
                pe.sem_inc(s_p, 2)
                pe.sem_inc(s_t, 2)

                def transpose(n, t):
                    pe.wait_ge(s_g, n + 1)
                    pe.wait_ge(s_c, n + 1)
                    for part in range(2):
                        for k in range(KT):
                            last = nc.tensor.transpose(tps[:, t, part, k * P:(k + 1) * P], og[:, t, part, k * P:(k + 1) * P],
                                                       kept["ident16"][:])
                    last.then_inc(s_t, 1)

                for n in range(2):
                    transpose(n, n)

                def body(j, r, ahead):
                    n, t = j * RX + r, r % 2
                    pe.wait_ge(s_c, n + 3)
                    pe.wait_ge(s_y1, n + 1)
                    for k in range(KT):
                        for i, (a, b) in enumerate(((0, "wo_head"), (0, "wo_tail"), (1, "wo_head"))):
                            last = nc.tensor.matmul(pso[:, t], oT[:, t, a, k], kept[b][:, k],
                                                    start=(k == 0 and i == 0), stop=(k == KT - 1 and i == 2))
                    last.then_inc(s_p, 1)
                    if ahead:
                        transpose(n + 2, t)
                turns(pe, body)

            @block.scalar
            def _(act):
                act.sem_inc(s_c, 2)

                def copy(n, t):
                    act.wait_ge(s_t, n + 3)
                    act.wait_ge(s_p, n + 1)
                    nc.scalar.activation(oT[:, t].rearrange("p a k n -> p (a k n)"), tps[:, t].rearrange("p a n -> p (a n)"),
                                         ACT.Copy).then_inc(s_c, 1)

                for n in range(2):
                    copy(n, n)

                def body(j, r, ahead):
                    n = j * RX + r
                    if ahead:
                        copy(n + 2, r % 2)
                turns(act, body)

            @block.gpsimd
            def _(pool):
                pool.sem_inc(s_y2, 2)
                with pool.Fori(0, TURNS) as j:
                    for r in range(RX):
                        n = j * RX + r
                        pool.wait_ge(s_y1, n + 3)
                        pool.wait_ge(s_y3, n + 1)
                        pool.wait_ge(ld[r], j * 32 + 32)
                        nc.gpsimd.tensor_tensor(y2[:, r % 2], y1[:, r % 2], gt[:, r], ALU.mult).then_inc(s_y2, 1)

            @block.vector
            def _(dve):
                dve.sem_inc(s_y1, 2)
                dve.sem_inc(s_y3, 2)

                def gather(j, r):
                    n, t = j * RX + r, r % 2
                    dve.wait_ge(s_t, n + 1)
                    bare(dve, s_bare)
                    for part in range(2):
                        heads = v_all[:, H * t:H * (t + 1), bass.ds(j * 2 + r // 2, 1), DH * part:DH * (part + 1)]
                        last = nc.vector.tensor_copy(og[:, t, part].rearrange("p (h d) -> p h d", h=H),
                                                     heads.rearrange("p h a d -> p (h a) d"))
                    last.then_inc(s_g, 1)

                def residual(j, r):
                    dve.wait_ge(s_y2, j * RX + (r + 3))
                    dve.wait_ge(ld[r], j * 32 + 32)
                    dve.wait_ge(st[r], j * 16 + 16)
                    nc.vector.scalar_tensor_tensor(y3[:, r], y2[:, r % 2], kept["ffn_scale"][:], xt[:, r],
                                                   ALU.mult, ALU.add).then_inc(s_y3, 1)

                gather(0, 0)
                gather(0, 1)

                def body(j, r, ahead):
                    if ahead:
                        gather(j + (r + 2) // RX, (r + 2) % RX)
                    n, t = j * RX + r, r % 2
                    dve.wait_ge(s_p, n + 3)
                    dve.wait_ge(s_y2, n + 1)
                    nc.vector.scalar_tensor_tensor(y1[:, t], pso[:, t], kept["out_scale"][:], kept["out_bias"][:],
                                                   ALU.mult, ALU.add).then_inc(s_y1, 1)
                    if r > 0:
                        residual(j, r - 1)
                    if r == RX - 1:
                        residual(j, r)
                turns(dve, body)


def build(nc, X, ln_g, ln_b, Wq, bq, Wk, bk, Wv, bv, Wo, bo, w_fc, w_proj, out):
    with ExitStack() as ctx:
        def sb(name, shape, dt):
            return ctx.enter_context(nc.sbuf_tensor(name, shape, dt))
        kept = dict(
            ident32=sb("ident32", [P, P], F32), ident16=sb("ident16", [P, P], F16), identb=sb("identb", [P, P], BF16),
            mask_kq=sb("mask_kq", [P, P], BF16), mask_qk=sb("mask_qk", [P, P], BF16),
            half=sb("half", [P, JT], F32),
            scale=sb("scale", [P, 4], F32), unscale=sb("unscale", [P, 4], F32),
            amean=sb("amean", [P, 2], F32), ffn_scale=sb("ffn_scale", [P, 1], F32), out_scale=sb("out_scale", [P, 1], F32),
            qk_bias=sb("qk_bias", [P, 2, KT], F32), out_bias=sb("out_bias", [P, D], F32),
            wo_head=sb("wo_head", [P, KT, D], F16), wo_tail=sb("wo_tail", [P, KT, D], F16),
            fc_T=sb("fc_T", [P, KT, HID], F16), proj_T=sb("proj_T", [P, HT, D], F16),
        )
        qk_dram = nc.dram_tensor("qk_split", (UNITS, 2, 2, DH, S), F16, kind="Internal").ap()
        xf_dram = nc.dram_tensor("xf_split", (NT // 2, P, 2, KT, 2 * P), F16, kind="Internal").ap()
        with ExitStack() as c2:
            kept["w_head"] = c2.enter_context(nc.sbuf_tensor("w_head", [P, 3, KT, D], F16))
            kept["w_tail"] = c2.enter_context(nc.sbuf_tensor("w_tail", [P, 3, KT, D], F16))
            weights_block(nc, (ln_g, ln_b, Wq, bq, Wk, bk, Wv, bv, Wo, bo, w_fc, w_proj), kept)
            kept["v_all"] = ctx.enter_context(nc.sbuf_tensor("v_all", [P, UNITS, S // P, VW], F16, side="right"))
            project_block(nc, X, qk_dram, xf_dram, kept)
        gate_dram = nc.dram_tensor("gate", (NT, P, D), F32, kind="Internal").ap()
        attend_block(nc, qk_dram, xf_dram, gate_dram, kept)
        finish_block(nc, X, out, gate_dram, kept)


_INS = ["L0_attn_X", "L0_attn_ln_g", "L0_attn_ln_b", "L0_attn_Wq", "L0_attn_bq", "L0_attn_Wk", "L0_attn_bk", "L0_attn_Wv",
        "L0_attn_bv", "L0_attn_Wo", "L0_attn_bo", "L0_ffn_w_fc", "L0_ffn_w_proj"]


def kernel(**inputs):
    import concourse.bacc as _bacc
    from concourse.bass_utils import run_bass_kernel_spmd as _run

    nc = _bacc.Bacc("TRN2", target_bir_lowering=False, num_devices=1)
    arrays, args = {}, []
    for name in _INS:
        a = np.ascontiguousarray(inputs[name])
        arrays[f"in_{name}"] = a
        args.append(nc.dram_tensor(f"in_{name}", a.shape, mybir.dt.from_np(a.dtype), kind="ExternalInput").ap())
    out = nc.dram_tensor("out_0", (B, S, D), F32, kind="ExternalOutput").ap()
    build(nc, *args, out)
    r = _run(nc, [arrays], core_ids=[0])
    return r.results[0]["out_0"]
```

```python
from contextlib import ExitStack

import numpy as np

import concourse.bass as bass
from concourse import mybir
from concourse.alu_op_type import AluOpType as ALU

ACT = mybir.ActivationFunctionType
F32 = mybir.dt.float32
F16 = mybir.dt.float16
BF16 = mybir.dt.bfloat16
I32 = mybir.dt.int32
AX = mybir.AxisListType

P = 128
B, S, D = 2, 2048, 512
H, DH = 16, 32
HID = 1280
KT = D // P
HT = HID // P
NT = B * S // P
G = 512
JT = G // P
CH = S // G
UNITS = B * H
EPS = 1e-5
BIG = 1e30
VW = 2 * DH + 1
V_SHIFT = 2.0 ** -9
RMAX = bass.bass_isa.ReduceOp.max
Q, K, V, O = range(4)


class Steps:

    def __init__(self, eng, sem, base=0):
        self.eng, self.sem, self.base, self.n = eng, sem, base, 0

    def did(self, instruction):
        instruction.then_inc(self.sem, 1)
        self.n += 1

    def settle(self):
        self.eng.wait_ge(self.sem, self.base + self.n)


def bare(eng, sem):
    eng.sem_inc(sem)


def weights_block(nc, x, ins, kept):
    (ln_g, ln_b, wq, bq, wk, bk, wv, bv, wo, bo, w_fc, w_proj) = ins
    with ExitStack() as ctx:
        def sb(name, shape, dt):
            return ctx.enter_context(nc.sbuf_tensor(name, shape, dt))

        def sem(name):
            return ctx.enter_context(nc.semaphore(name))

        raw_v, raw_o = sb("wv_raw", [P, KT, D], F32), sb("wo_raw", [P, KT, D], F32)
        wf = [kept["xin"][:, 0], kept["xin"][:, 1], raw_v, raw_o]
        wg = sb("w_gained", [P, 3, KT, D], F32)
        fc = sb("w_fc_raw", [P, HT, D], F32)
        pr = sb("w_proj_raw", [P, KT, HID], F32)
        fc_lt = sb("fc_lt", [P, HT, D], F16)
        pr_lt = sb("pr_lt", [P, KT, HID], F16)
        fc_gt = sb("fc_gt", [P, HT, D], F16)
        pr_gt = sb("pr_gt", [P, KT, HID], F16)
        minus16 = sb("minus_ident16", [P, P], F16)
        vecs = sb("vectors", [P, 5, KT], F32)
        bo_row = sb("bo_row", [P, D], F32)
        amax = sb("amax", [P, 4], F32)
        gmax = sb("gmax", [P, 4], F32)
        pw = sb("pw", [P, 4], F32)
        rpw = sb("rpw", [P, 4], F32)
        asum = sb("asum", [P, 2], F32)
        thr = sb("thr", [P, 2], F32)
        minus_thr = sb("minus_thr", [P, 2], F32)
        am2 = sb("am2", [P, 2], F32)
        ones = sb("ones", [P, P], F32)
        vb = sb("v_bias", [P, KT], F32)
        vb_wide = sb("v_bias_wide", [P, KT, P], F32)

        tp = ctx.enter_context(nc.psum_tensor("w_tp", [P, 4, 512], F32))
        pb = ctx.enter_context(nc.psum_tensor("w_bias", [P, 512], F32))
        ps = ctx.enter_context(nc.psum_tensor("w_sum", [P, 2, 512], F32))
        po = ctx.enter_context(nc.psum_tensor("w_obias", [P, 512], F32))

        ld_w = [sem(f"ld_w{m}") for m in range(4)]
        ld_vec = sem("ld_vec")
        ld_x = sem("ld_x_first")
        ld_fc, ld_pr, ld_bo = sem("ld_fc"), sem("ld_pr"), sem("ld_bo")
        s_pool = sem("s_pool")
        s_ones = sem("s_ones")
        s_amax = sem("s_amax")
        s_gmax = sem("s_gmax")
        s_scale = sem("s_scale")
        s_head = sem("s_head")
        s_asum = sem("s_asum")
        s_sum = sem("s_sum")
        s_tern = sem("s_tern")
        s_tp, s_tc = sem("s_tp"), sem("s_tc")
        s_bias = sem("s_bias")
        s_vbw = sem("s_vbw")
        s_obias = sem("s_obias")
        s_dve = sem("s_dve")

        with nc.Block() as block:
            @block.sync
            def _(sp):
                for m, w in enumerate((wq, wk, wv)):
                    sp.dma_start(wf[m][:], w.rearrange("(k p) n -> p k n", p=P)).then_inc(ld_w[m], 16)
                with nc.allow_non_contiguous_dma(reason="five short vectors as columns"):
                    for n, v in enumerate((ln_g, ln_b, bq, bk, bv)):
                        sp.dma_start(vecs[:, n], v.rearrange("(k p) -> p k", p=P)).then_inc(ld_vec, 16)
                sp.dma_start(wf[O][:], wo.rearrange("(k p) n -> p k n", p=P)).then_inc(ld_w[O], 16)
                sp.dma_start(fc[:], w_fc.rearrange("(k p) n -> p k n", p=P)).then_inc(ld_fc, 16)
                sp.dma_start(pr[:], w_proj.rearrange("(k p) n -> p k n", p=P)).then_inc(ld_pr, 16)
                sp.dma_start(bo_row[:], bo.rearrange("(a n) -> a n", a=1).to_broadcast([P, D])).then_inc(ld_bo, 16)
                sp.wait_ge(s_amax, 2)
                sp.wait_ge(s_bias, 1)
                for u in range(2):
                    sp.dma_start(kept["xin"][:, u], x[u, 0:G, :].rearrange("(j p) d -> p j d", p=P)).then_inc(ld_x, 16)
                sp.wait_ge(ld_x, 32)

            @block.gpsimd
            def _(pool):
                own = Steps(pool, s_pool)
                own.did(nc.gpsimd.memset(ones[:], 1.0))
                for t in (kept["ident32"], kept["ident16"], kept["identb"], kept["mask_kq"], kept["mask_qk"]):
                    own.did(nc.gpsimd.memset(t[:], 0.0))
                own.did(nc.gpsimd.memset(kept["half"][:], -0.5))
                own.did(nc.gpsimd.memset(minus16[:], 0.0))
                own.settle()
                for t in (kept["ident32"], kept["ident16"], kept["identb"]):
                    nc.gpsimd.affine_select(out=t[:], in_=t[:], compare_op=ALU.not_equal, fill=1.0, base=0,
                                            pattern=[[-1, P]], channel_multiplier=1).then_inc(s_ones, 1)
                nc.gpsimd.affine_select(out=minus16[:], in_=minus16[:], compare_op=ALU.not_equal, fill=-1.0, base=0,
                                        pattern=[[-1, P]], channel_multiplier=1).then_inc(s_ones, 1)
                nc.gpsimd.affine_select(out=kept["mask_kq"][:], in_=kept["mask_kq"][:], compare_op=ALU.is_ge, fill=-BIG,
                                        base=0, pattern=[[1, P]], channel_multiplier=-1).then_inc(s_ones, 1)
                nc.gpsimd.affine_select(out=kept["mask_qk"][:], in_=kept["mask_qk"][:], compare_op=ALU.is_ge, fill=-BIG,
                                        base=0, pattern=[[-1, P]], channel_multiplier=1).then_inc(s_ones, 1)
                for m in range(4):
                    pool.wait_ge(s_amax, m + 1)
                    nc.gpsimd.partition_all_reduce(gmax[:, m:m + 1], amax[:, m:m + 1], P, RMAX).then_inc(s_gmax, 1)

            @block.scalar
            def _(act):
                def head(m):
                    act.wait_ge(s_scale, m + 1)
                    src = wg[:, m] if m < 3 else wf[O][:]
                    nc.scalar.activation(kept["w_head"][:, m] if m < 3 else kept["wo_head"][:], src, ACT.Identity,
                                         scale=kept["scale"][:, m:m + 1]).then_inc(s_head, 1)

                def absolute_sum(c):
                    ld, raw, to = ((ld_fc, fc, fc_gt), (ld_pr, pr, pr_gt))[c]
                    act.wait_ge(ld, 16)
                    nc.scalar.activation(to[:].rearrange("p a b -> p (a b)"), raw[:].rearrange("p a b -> p (a b)"), ACT.Abs,
                                         accum_out=asum[:, c:c + 1]).then_inc(s_asum, 1)

                for m in range(3):
                    head(m)
                absolute_sum(0)
                head(O)
                absolute_sum(1)
                for n in range(20):
                    act.wait_ge(s_tp, n + 1)
                    if n < 10:
                        dst = kept["fc_T"][:, :, n * P:(n + 1) * P]
                    else:
                        dst = kept["proj_T"][:, n - 10, :].rearrange("p (k n) -> p k n", k=KT)
                    nc.scalar.activation(dst, tp[:, n % 4].rearrange("p (k n) -> p k n", k=4), ACT.Copy).then_inc(s_tc, 1)

            @block.vector
            def _(dve):
                own = Steps(dve, s_dve)

                def scales(m):
                    dve.wait_ge(s_gmax, m + 1)
                    c = slice(m, m + 1)
                    own.did(nc.vector.tensor_scalar(gmax[:, c], gmax[:, c], 1e-30, None, ALU.max))
                    own.settle()
                    own.did(nc.vector.tensor_single_scalar(pw[:, c].bitcast(I32), gmax[:, c].bitcast(I32), 0x7F800000, ALU.bitwise_and))
                    own.settle()
                    own.did(nc.vector.reciprocal(rpw[:, c], pw[:, c]))
                    own.settle()
                    own.did(nc.vector.tensor_scalar(kept["scale"][:, c], rpw[:, c], 2.0 ** 14, None, ALU.mult))
                    own.settle()
                    nc.vector.tensor_scalar(kept["unscale"][:, c], pw[:, c], 2.0 ** -14, None, ALU.mult).then_inc(s_scale, 1)

                def tail(m):
                    dve.wait_ge(s_head, m + 1)
                    src = wg[:, m] if m < 3 else wf[O][:]
                    hi, lo = (kept["w_head"][:, m], kept["w_tail"][:, m]) if m < 3 else (kept["wo_head"][:], kept["wo_tail"][:])
                    own.did(nc.vector.scalar_tensor_tensor(lo, src, kept["scale"][:, m:m + 1], hi, ALU.mult, ALU.subtract))

                dve.wait_ge(ld_vec, 80)
                for m in range(3):
                    dve.wait_ge(ld_w[m], 16)
                    for k in range(KT):
                        own.did(nc.vector.tensor_scalar(wg[:, m, k], wf[m][:, k], vecs[:, 0, k:k + 1], None, ALU.mult))
                    own.settle()
                    nc.vector.tensor_reduce(amax[:, m:m + 1], wg[:, m], AX.XY, ALU.max, apply_absolute_value=True).then_inc(s_amax, 1)
                    if m:
                        scales(m - 1)
                        if m > 1:
                            tail(m - 2)
                scales(2)
                tail(1)
                dve.wait_ge(ld_w[O], 16)
                nc.vector.tensor_reduce(amax[:, O:O + 1], wf[O][:], AX.XY, ALU.max, apply_absolute_value=True).then_inc(s_amax, 1)
                tail(2)
                scales(O)
                dve.wait_ge(s_bias, 1)
                bc = pb[:, 0:12].rearrange("p (m k) -> p m k", m=3)
                own.did(nc.vector.tensor_tensor(kept["qk_bias"][:], bc[:, 0:2], vecs[:, 2:4], ALU.add))
                own.did(nc.vector.tensor_tensor(vb[:], bc[:, 2], vecs[:, 4], ALU.add))
                own.settle()
                nc.vector.tensor_copy(vb_wide[:], vb[:].rearrange("p (k a) -> p k a", a=1).to_broadcast([P, KT, P])).then_inc(s_vbw, 1)
                tail(O)
                for raw, gt, lt, c in ((fc, fc_gt, fc_lt, 0), (pr, pr_gt, pr_lt, 1)):
                    one = slice(c, c + 1)
                    dve.wait_ge(s_sum, c + 1)
                    own.did(nc.vector.tensor_scalar(kept["amean"][:, one], ps[:, c, 0:1], 1.0 / (HID * D), 1e-5, ALU.mult, ALU.max))
                    own.settle()
                    own.did(nc.vector.tensor_scalar(thr[:, one], kept["amean"][:, one], 0.7, None, ALU.mult))
                    own.settle()
                    own.did(nc.vector.tensor_scalar(minus_thr[:, one], thr[:, one], -1.0, None, ALU.mult))
                    own.settle()
                    nc.vector.tensor_scalar(gt[:], raw[:], thr[:, one], None, ALU.is_gt).then_inc(s_tern, 1)
                    nc.vector.tensor_scalar(lt[:], raw[:], minus_thr[:, one], None, ALU.is_lt).then_inc(s_tern, 1)
                own.did(nc.vector.tensor_tensor(am2[:, 0:1], kept["amean"][:, 0:1], kept["amean"][:, 0:1], ALU.mult))
                own.settle()
                own.did(nc.vector.tensor_tensor(am2[:, 1:2], am2[:, 0:1], kept["amean"][:, 1:2], ALU.mult))
                own.settle()
                own.did(nc.vector.tensor_scalar(kept["ffn_scale"][:], am2[:, 1:2], 8.0, None, ALU.mult))
                own.did(nc.vector.scalar_tensor_tensor(kept["out_scale"][:], kept["unscale"][:, V:V + 1], 1.0 / V_SHIFT,
                                                       kept["unscale"][:, O:O + 1], ALU.mult, ALU.mult))
                dve.wait_ge(s_obias, 1)
                dve.wait_ge(ld_bo, 16)
                own.did(nc.vector.tensor_tensor(kept["out_bias"][:], po[:], bo_row[:], ALU.add))

            @block.tensor
            def _(pe):
                pe.wait_ge(ld_vec, 80)
                for m in range(3):
                    pe.wait_ge(ld_w[m], 16)
                    for mt in range(KT):
                        for k in range(KT):
                            last = nc.tensor.matmul(pb[:, 4 * m + mt:4 * m + mt + 1], wf[m][:, k, mt * P:(mt + 1) * P],
                                                    vecs[:, 1, k:k + 1], start=(k == 0), stop=(k == KT - 1))
                last.then_inc(s_bias, 1)

                def whole_sum(c):
                    pe.wait_ge(s_asum, c + 1)
                    nc.tensor.matmul(ps[:, c, 0:1], ones[:], asum[:, c:c + 1], start=True, stop=True).then_inc(s_sum, 1)

                pe.wait_ge(s_pool, 8)
                pe.wait_ge(s_ones, 6)
                whole_sum(0)
                pe.wait_ge(s_vbw, 1)
                pe.wait_ge(ld_w[O], 16)
                for k in range(KT):
                    last = nc.tensor.matmul(po[:], vb_wide[:, k], wf[O][:, k], start=(k == 0), stop=(k == KT - 1))
                last.then_inc(s_obias, 1)
                whole_sum(1)
                for n in range(20):
                    if n % 10 == 0:
                        pe.wait_ge(s_tern, n // 10 * 2 + 2)
                    if n >= 4:
                        pe.wait_ge(s_tc, n - 3)
                    for k in range(4):
                        for src, ident in ((fc_gt if n < 10 else pr_gt, kept["ident16"]), (fc_lt if n < 10 else pr_lt, minus16)):
                            tile_ = src[:, n, k * P:(k + 1) * P] if n < 10 else src[:, k, (n - 10) * P:(n - 9) * P]
                            last = nc.tensor.matmul(tp[:, n % 4, k * P:(k + 1) * P], tile_, ident[:],
                                                    start=(src in (fc_gt, pr_gt)), stop=(src in (fc_lt, pr_lt)))
                    last.then_inc(s_tp, 1)


QB = S // P
NG = S // G


def maximum_rounds():
    return [(i, c, min(G, (i + 1) * P - c * G)) for i in range(QB) for c in range(i // JT + 1)]


ROUNDS = maximum_rounds()
NR = len(ROUNDS)


def load_score_operands(eng, qk_dram, unit, q_to, k_to, semaphore):
    src = qk_dram[bass.ds(unit, 1)]
    hd_tl = lambda m: src[:, m].rearrange("a t d s -> (a t d) s")
    hd = lambda m: src[:, m, 0].rearrange("a d s -> (a d) s")
    eng.dma_start(q_to[0:64, :], hd_tl(0)).then_inc(semaphore, 16)
    eng.dma_start(q_to[64:96, :], hd(0)).then_inc(semaphore, 16)
    eng.dma_start(k_to[0:32, :], hd(1)).then_inc(semaphore, 16)
    eng.dma_start(k_to[32:96, :], hd_tl(1)).then_inc(semaphore, 16)


def round_scores(nc, bank, q, k, kept, r):
    i, c, w = ROUNDS[r]
    diagonal = c == i // JT
    last = nc.tensor.matmul(bank[:, 0:w], q[0:96, i * P:(i + 1) * P], k[0:96, c * G:c * G + w], start=True, stop=not diagonal)
    if diagonal:
        last = nc.tensor.matmul(bank[:, w - P:w], kept["identb"][:], kept["mask_qk"][:], start=False, stop=True)
    return last


def round_maximum(nc, bank, mx, r):
    i, c, w = ROUNDS[r]
    return nc.vector.tensor_reduce(mx[:, c, i:i + 1], bank[:, 0:w], AX.X, ALU.max)


T_PER, PJ_PER, QK_PER = 2 * JT, 3 * KT, 2 * KT
AFTER = 3
RING = 4
GROUPS = B * CH


def project_block(nc, x, qk_dram, xf_dram, kept):
    with ExitStack() as ctx:
        def sb(name, shape, dt):
            return ctx.enter_context(nc.sbuf_tensor(name, shape, dt))

        def sem(name):
            return ctx.enter_context(nc.semaphore(name))

        xin = kept["xin"]
        xn = sb("xn", [P, JT, D], F32)
        xn2 = sb("xn2", [P, JT, D], F32)
        st6 = sb("st6", [P, JT, 6], F32)
        mv = sb("mv", [P, JT, 2], F32)
        var1 = sb("var1", [P, JT], F32)
        r1 = sb("r1", [P, JT], F32)
        var1_r = sb("var1_r", [P, JT], F32)
        var2 = sb("var2", [P, JT], F32)
        var2_eps = sb("var2_eps", [P, JT], F32)
        r2 = sb("r2", [P, JT], F32)
        f_head = sb("f_head", [P, 2, KT, G], F16)
        f_tail = sb("f_tail", [P, 2, KT, G], F16)
        a_head = sb("a_head", [P, 2, KT, G], F16)
        a_tail = sb("a_tail", [P, 2, KT, G], F16)
        qk32 = sb("qk32", [P, RING, G], F32)
        qk_head = sb("qk_head", [P, RING, G], F16)
        qk_tail = sb("qk_tail", [P, RING, G], F16)
        tps = ctx.enter_context(nc.psum_tensor("tps", [P, RING, 512], F32))
        pjs = ctx.enter_context(nc.psum_tensor("pjs", [P, RING, 512], F32))
        v_all = kept["v_all"]

        ld_x = [sem(f"ld_x{u}") for u in range(2)]
        s_var1, s_r1, s_var2, s_r2 = sem("s_var1"), sem("s_r1"), sem("s_var2"), sem("s_r2")
        s_xn, s_xn2 = sem("s_xn"), sem("s_xn2")
        s_v_ones = sem("s_v_ones")
        s_bare = sem("s_bare")
        s_own = sem("s_own")
        s_t = sem("s_t")
        s_th, s_tt = sem("s_th"), sem("s_tt")
        s_pj = sem("s_pj")
        s_pa = sem("s_pa")
        s_ph = sem("s_ph")
        s_pt = sem("s_pt")
        st_qk = [sem(f"st_qk{r}") for r in range(RING)]
        st_xf = [sem(f"st_xf{u}") for u in range(2)]

        q_mx, k_mx = f_head[:, 0].rearrange("p k n -> p (k n)"), f_tail[:, 0].rearrange("p k n -> p (k n)")
        mx = kept["mx"]
        ld_mx = sem("ld_mx_first")
        s_unset = sem("s_unset")
        s_mx, s_mr = sem("s_mx_first"), sem("s_mr_first")

        def rounds_after(i):
            return range(NR * max(i - 1, 0) // (PJ_PER - 2), min(NR, NR * i // (PJ_PER - 2)))

        OWN_PER = 2 * JT + 2

        def groups(eng, body):
            with eng.Fori(0, CH - 1) as it:
                for u in range(2):
                    body(it * 2 + u, it, u, True)
            for u in range(2):
                body(GROUPS - 2 + u, CH - 1, u, u == 0)

        def nxt(it, u):
            return (it, 1) if u == 0 else (it + 1, 0)

        with nc.Block() as block:
            @block.sync
            def _(sp):
                for r in range(RING):
                    sp.sem_inc(st_qk[r], 32)
                for u in range(2):
                    sp.sem_inc(st_xf[u], 64)

                def load_x(it, u):
                    sp.dma_start(xin[:, u], x[u, bass.ds(it * G, G), :].rearrange("(j p) d -> p j d", p=P)).then_inc(ld_x[u], 16)

                def store_xf(it, u):
                    for h in range(2):
                        for part, src in enumerate((f_head, f_tail)):
                            sp.dma_start(xf_dram[bass.ds(it * 2 + (8 * u + h), 1), :, part],
                                         src[:, u, :, 256 * h:256 * (h + 1)]).then_inc(st_xf[u], 16)

                for u in range(2):
                    sp.sem_inc(ld_x[u], 16)
                sp.wait_ge(s_tt, T_PER)
                store_xf(0, 0)

                def body(g, it, u, more):
                    if more and not (isinstance(it, int) and it == CH - 1):
                        sp.wait_ge(s_xn, g * JT + JT)
                        load_x(it + 1, u)
                    if not more:
                        for r in range(RING):
                            sp.wait_ge(st_qk[r], 32 + 32 * (GROUPS - 1) * QK_PER // RING)
                        sp.wait_ge(st_xf[0], 64 + 64 * CH)
                        load_score_operands(sp, qk_dram, 0, q_mx, k_mx, ld_mx)
                    for i in range(QK_PER):
                        sp.wait_ge(s_pt, g * PJ_PER + (RING + i + 1))
                        for part, src in enumerate((qk_head, qk_tail)):
                            first = 16 * u + 4 * (i % KT)
                            sp.dma_start(qk_dram[first:first + 4, i // KT, part, :, bass.ds(it * G, G)],
                                         src[:, i % RING]).then_inc(st_qk[i % RING], 16)
                    if more:
                        sp.wait_ge(s_tt, g * T_PER + 2 * T_PER)
                        store_xf(*nxt(it, u))
                groups(sp, body)
                for r in range(RING):
                    sp.wait_ge(st_qk[r], 32 + 32 * GROUPS * QK_PER // RING)
                for u in range(2):
                    sp.wait_ge(st_xf[u], 64 + 64 * CH)

            @block.gpsimd
            def _(pool):
                def norms(g):
                    pool.wait_ge(s_var1, g + 1)
                    nc.gpsimd.tensor_tensor(r1[:], var1[:], kept["half"][:], ALU.pow).then_inc(s_r1, 1)
                    pool.wait_ge(s_var2, g + 1)
                    nc.gpsimd.tensor_tensor(r2[:], var2_eps[:], kept["half"][:], ALU.pow).then_inc(s_r2, 1)

                def second(g, first):
                    pool.wait_ge(s_r2, g + 1)
                    for j in range(JT):
                        pool.wait_ge(s_xn, g * JT + (j + 1))
                        if not first:
                            pool.wait_ge(s_t, g * T_PER + (2 * j + 2 - T_PER))
                        bare(pool, s_bare)
                        nc.gpsimd.tensor_scalar(xn2[:, j], xn[:, j], r2[:, j:j + 1], 1.0, ALU.mult, ALU.mult).then_inc(s_xn2, 1)

                norms(0)
                second(0, True)
                nc.gpsimd.memset(v_all[:, :, :, 2 * DH:VW], 1.0).then_inc(s_v_ones, 1)

                def body(g, it, u, more):
                    if more:
                        norms(g + 1)
                        second(g + 1, False)
                    for i in range(QK_PER):
                        pool.wait_ge(s_pa, g * PJ_PER + (RING + i + 1))
                        pool.wait_ge(st_qk[i % RING], g * (32 * QK_PER // RING) + (32 * (i // RING) + 32))
                        bare(pool, s_bare)
                        nc.gpsimd.tensor_scalar(qk_head[:, i % RING], qk32[:, i % RING], 1.0, 0.0, ALU.mult, ALU.add).then_inc(s_ph, 1)
                groups(pool, body)

            @block.scalar
            def _(act):
                act.sem_inc(s_pa, RING)

                def head(g, i, it, u):
                    act.wait_ge(s_t, g * T_PER + (i + 1))
                    if i == 0:
                        act.wait_ge(st_xf[u], it * 64 + 64)
                    dst = f_head if i % 2 == 0 else a_head
                    nc.scalar.activation(dst[:, u, :, P * (i // 2):P * (i // 2 + 1)],
                                         tps[:, i % RING].rearrange("p (k n) -> p k n", k=KT), ACT.Copy).then_inc(s_th, 1)

                for i in range(T_PER):
                    head(0, i, 0, 0)

                def body(g, it, u, more):
                    for i in range(PJ_PER):
                        act.wait_ge(s_pj, g * PJ_PER + (i + 1))
                        if i < QK_PER:
                            act.wait_ge(s_pt, g * PJ_PER + (i + 1))
                            m, mt = divmod(i, KT)
                            nc.scalar.activation(qk32[:, i % RING], pjs[:, i % RING], ACT.Identity,
                                                 scale=kept["unscale"][:, m:m + 1],
                                                 bias=kept["qk_bias"][:, m, mt:mt + 1]).then_inc(s_pa, 1)
                        else:
                            nc.scalar.activation(v_all[:, H * u:H * (u + 1), bass.ds(it * JT + (i - QK_PER), 1), DH:2 * DH],
                                                 pjs[:, i % RING].rearrange("p (h a d) -> p h a d", a=1, h=H), ACT.Copy,
                                                 scale=V_SHIFT).then_inc(s_pa, 1)
                        if more and 0 <= i - AFTER < T_PER:
                            head(g + 1, i - AFTER, *nxt(it, u))
                groups(act, body)

            @block.vector
            def _(dve):
                dve.sem_inc(s_pt, RING)
                for c in range(1, NG):
                    nc.vector.memset(mx[:, c, 0:JT * c], -BIG).then_inc(s_unset, 1)
                dve.wait_ge(s_unset, NG - 1)

                def norms(g, it, u, first):
                    own = Steps(dve, s_own, g * OWN_PER)
                    dve.wait_ge(ld_x[u], it * 16 + 16)
                    for j in range(JT):
                        own.did(nc.vector.bn_stats(st6[:, j], xin[:, u, j]))
                    own.settle()
                    bare(dve, s_bare)
                    for j in range(JT):
                        own.did(nc.vector.bn_aggr(mv[:, j], st6[:, j]))
                    own.settle()
                    nc.vector.tensor_scalar(var1[:], mv[:, :, 1], EPS, None, ALU.add).then_inc(s_var1, 1)
                    dve.wait_ge(s_r1, g + 1)
                    for j in range(JT):
                        if not first:
                            dve.wait_ge(s_t, g * T_PER + (2 * j + 1 - T_PER))
                            dve.wait_ge(s_xn2, g * JT + (j + 1 - JT))
                        nc.vector.tensor_scalar(xn[:, j], xin[:, u, j], mv[:, j, 0:1], r1[:, j:j + 1],
                                                ALU.subtract, ALU.mult).then_inc(s_xn, 1)
                        if j == 0:
                            own.did(nc.vector.tensor_tensor(var1_r[:], mv[:, :, 1], r1[:], ALU.mult))
                            own.settle()
                            own.did(nc.vector.tensor_tensor(var2[:], var1_r[:], r1[:], ALU.mult))
                            own.settle()
                            nc.vector.tensor_scalar(var2_eps[:], var2[:], EPS, None, ALU.add).then_inc(s_var2, 1)
                    assert own.n == OWN_PER

                def tail(g, i, u):
                    dve.wait_ge(s_th, g * T_PER + (i + 1))
                    hi, lo = (f_head, f_tail) if i % 2 == 0 else (a_head, a_tail)
                    c = slice(P * (i // 2), P * (i // 2 + 1))
                    nc.vector.tensor_tensor(lo[:, u, :, c], tps[:, i % RING].rearrange("p (k n) -> p k n", k=KT),
                                            hi[:, u, :, c], ALU.subtract).then_inc(s_tt, 1)

                norms(0, 0, 0, True)
                for i in range(T_PER):
                    tail(0, i, 0)

                def body(g, it, u, more):
                    if more:
                        norms(g + 1, *nxt(it, u), False)
                    for i in range(PJ_PER):
                        if i < QK_PER:
                            dve.wait_ge(s_ph, g * QK_PER + (i + 1))
                            nc.vector.tensor_tensor(qk_tail[:, i % RING], qk32[:, i % RING], qk_head[:, i % RING],
                                                    ALU.subtract).then_inc(s_pt, 1)
                        else:
                            dve.wait_ge(s_pa, g * PJ_PER + (RING + i + 1))
                            vt = v_all[:, H * u:H * (u + 1), bass.ds(it * JT + (i - QK_PER), 1), :].rearrange("p h a d -> p (h a) d")
                            nc.vector.scalar_tensor_tensor(vt[:, :, 0:DH], pjs[:, i % RING].rearrange("p (h d) -> p h d", h=H),
                                                           V_SHIFT, vt[:, :, DH:2 * DH], ALU.mult, ALU.subtract).then_inc(s_pt, 1)
                        if more and 0 <= i - AFTER < T_PER:
                            tail(g + 1, i - AFTER, nxt(it, u)[1])
                        if not more:
                            for r in rounds_after(i):
                                dve.wait_ge(s_mx, r + 1)
                                round_maximum(nc, tps[:, r % RING], mx, r).then_inc(s_mr, 1)
                groups(dve, body)

            @block.tensor
            def _(pe):
                def transpose(g, i, first):
                    j = i // 2
                    pe.wait_ge(s_xn if i % 2 == 0 else s_xn2, g * JT + (j + 1))
                    if not (first and i < RING):
                        pe.wait_ge(s_tt, g * T_PER + (i + 1 - RING))
                    src = xn if i % 2 == 0 else xn2
                    for k in range(KT):
                        last = nc.tensor.transpose(tps[:, i % RING, k * P:(k + 1) * P], src[:, j, k * P:(k + 1) * P],
                                                   kept["ident32"][:])
                    last.then_inc(s_t, 1)

                for i in range(T_PER):
                    transpose(0, i, True)

                wh, wt = kept["w_head"], kept["w_tail"]

                def body(g, it, u, more):
                    pe.wait_ge(s_tt, g * T_PER + T_PER)
                    for i in range(PJ_PER):
                        pe.wait_ge(s_pa, g * PJ_PER + (i + 1))
                        pe.wait_ge(s_pt, g * PJ_PER + (i + 1))
                        m, mt = divmod(i, KT)
                        for k in range(KT):
                            ws = slice(mt * P, (mt + 1) * P)
                            if m < V:
                                pairs = [(wh[:, m, k, ws], a_head[:, u, k]), (wh[:, m, k, ws], a_tail[:, u, k]),
                                         (wt[:, m, k, ws], a_head[:, u, k])]
                            else:
                                pairs = [(a_head[:, u, k, ws], wh[:, m, k]), (a_head[:, u, k, ws], wt[:, m, k]),
                                         (a_tail[:, u, k, ws], wh[:, m, k])]
                            for n, (a, b) in enumerate(pairs):
                                last = nc.tensor.matmul(pjs[:, i % RING], a, b, start=(k == 0 and n == 0),
                                                        stop=(k == KT - 1 and n == 2))
                        last.then_inc(s_pj, 1)
                        if more and 0 <= i - AFTER < T_PER:
                            transpose(g + 1, i - AFTER, False)
                        if not more:
                            for r in rounds_after(i):
                                if r == 0:
                                    pe.wait_ge(ld_mx, 64)
                                if r >= RING:
                                    pe.wait_ge(s_mr, r + 1 - RING)
                                round_scores(nc, tps[:, r % RING], q_mx, k_mx, kept, r).then_inc(s_mx, 1)
                groups(pe, body)


LAG = 5
TAIL_LAG = LAG - 2
HD_RING, TL_RING, W_RING = 8, 5, 5
SHIFT = HD_RING
AV_CREDIT = 4
MX_LEAD = 28
POOL_SHARE = (0.4, 0.6)
P_SHIFT = 10
SCALE = DH ** -0.5
FT = 2 * P


def attention_steps():
    steps = []
    for g in range(NG):
        for j in range(0, JT * (g + 1), 2):
            parts, at = [], 0
            for key in (j, j + 1):
                q0 = max(0, key - JT * g) * P
                parts.append((key, q0, at))
                at += G - q0
            steps.append((g, parts, at))
    return steps


STEPS = attention_steps()
NS = len(STEPS)
assert NR == 2 * NS
POOL_COLS = [[int(cols * share) // 32 * 32 for _, _, cols in STEPS] for share in POOL_SHARE]
F1_AT = {1 + 2 * m: m for m in range(HT)}
F2_AT = {22 + c: (0, c) for c in range(5)} | {30 + c: (1, c) for c in range(5)}


def attend_block(nc, qk_dram, xf_dram, gate_dram, kept):
    with ExitStack() as ctx:
        def sb(name, shape, dt):
            return ctx.enter_context(nc.sbuf_tensor(name, shape, dt))

        def sem(name):
            return ctx.enter_context(nc.semaphore(name))

        q_mx = [sb(f"q_mx{u}", [P, S], F16) for u in range(2)]
        k_mx = [sb(f"k_mx{u}", [P, S], F16) for u in range(2)]
        q_st = [sb(f"q_st{u}", [P, S], F16) for u in range(2)]
        k_st = [sb(f"k_st{u}", [P, S], F16) for u in range(2)]
        w32 = sb("w32", [P, W_RING, 2 * G], F32)
        w_hd = sb("w_hd", [P, HD_RING, 2 * G], F16)
        w_tl = sb("w_tl", [P, TL_RING, 2 * G], F16)
        v_st = sb("v_st", [P, 2, QB, VW], F16)
        mx = kept["mx"]
        mm = sb("mm", [P, QB], F32)
        mneg = sb("mneg", [P, QB], F32)
        m_ht = sb("m_ht", [P, 2, QB], F16)
        m_rows = sb("m_rows", [2 * QB, P], F16)
        o_raw = sb("o_raw", [P, 2, QB, VW], F32)
        rden = sb("rden", [P, QB], F32)
        xf = sb("xf", [P, 2, KT, FT], F16)
        r32 = sb("r32", [P, 2, FT], F32)
        s_hd = sb("s_hd", [P, HT, FT], F16)
        s_tl = sb("s_tl", [P, HT, FT], F16)
        g32 = sb("g32", [P, 2, D], F32)
        st_ps = ctx.enter_context(nc.psum_tensor("st_ps", [P, 2, 2 * G], F32))
        mx_ps = ctx.enter_context(nc.psum_tensor("mx_ps", [P, 2, G], F32))
        av_ps = ctx.enter_context(nc.psum_tensor("av_ps", [P, G], F32))
        ff_ps = ctx.enter_context(nc.psum_tensor("ff_ps", [P, D], F32))
        av = av_ps[:, 0:JT * VW].rearrange("p (i v) -> p i v", i=JT)
        v_all = kept["v_all"]

        ld_mx = [sem(f"ld_mx{u}") for u in range(2)]
        ld_st = [sem(f"ld_st{u}") for u in range(2)]
        ld_mr = [sem(f"ld_mr{u}") for u in range(2)]
        ld_xf = sem("ld_xf")
        st_g = [sem(f"st_g{u}") for u in range(2)]
        s_set = sem("s_set")
        s_st = sem("s_st")
        s_exp = sem("s_exp")
        s_head = sem("s_head_a")
        s_tld = sem("s_tld")
        s_tlp = sem("s_tlp")
        s_av = sem("s_av")
        s_avc = sem("s_avc")
        s_vs = sem("s_vs")
        s_mx = sem("s_mx")
        s_mr = sem("s_mr")
        s_m = sem("s_m")
        s_mh = sem("s_mh")
        s_tm = sem("s_tm")
        s_row = sem("s_row")
        s_rd = sem("s_rd")
        s_os = sem("s_os")
        s_on = sem("s_on")
        s_oh = sem("s_oh")
        s_ot = sem("s_ot")
        s_f1 = sem("s_f1")
        s_re = sem("s_re")
        s_sq = sem("s_sq")
        s_sh = sem("s_sh")
        s_sl = sem("s_sl")
        s_f2 = sem("s_f2")
        s_e = sem("s_e")
        s_ga = sem("s_ga")
        s_bare = sem("s_bare_a")

        PAIRS = UNITS // 2
        N2 = 2 * NS

        def place(it, n):
            return it * 2 + n // NS, (n // NS) % 2, it + n // N2, n % NS

        def split_done(eng, count):
            eng.wait_ge(s_tlp, count)
            eng.wait_ge(s_tld, count)

        def exists(it, n):
            return not (isinstance(it, int) and it * N2 + n >= UNITS * NS)

        def before(it, n, k):
            return isinstance(it, int) and it * N2 + n < k

        def pairs(eng, body):
            with eng.Fori(0, PAIRS - 1) as it:
                body(it)
            body(PAIRS - 1)

        def all_steps(eng, step):
            for n in range(SHIFT):
                step(0, n)
            with eng.Fori(0, PAIRS - 1) as it:
                for n in range(SHIFT, SHIFT + N2):
                    step(it, n)
            for n in range(SHIFT, N2):
                step(PAIRS - 1, n)

        with nc.Block() as block:
            @block.sync
            def _(sp):
                for u in range(2):
                    sp.sem_inc(st_g[u], 16)

                def load_operands(unit, q_to, k_to, semaphore):
                    load_score_operands(sp, qk_dram, unit, q_to, k_to, semaphore)

                def store_rows(unit, u):
                    sp.wait_ge(s_row, unit + 1)
                    for t in range(2):
                        sp.dma_start(q_st[u][96 + t:97 + t, :].rearrange("a (i c) -> a i c", i=QB),
                                     m_rows[QB * t:QB * (t + 1), :]).then_inc(ld_mr[u], 16)

                sp.sem_inc(ld_mx[0], 64)
                load_operands(1, q_mx[1], k_mx[1], ld_mx[1])
                load_operands(0, q_st[0], k_st[0], ld_st[0])
                sp.dma_start(xf[:], xf_dram[0]).then_inc(ld_xf, 16)
                store_rows(0, 0)

                def store_gates(it):
                    for t in range(2):
                        sp.wait_ge(s_ga, it * 2 + (t + 2))
                        sp.dma_start(gate_dram[bass.ds(it * 2 + t, 1)].rearrange("a p d -> (a p) d"), g32[:, t]).then_inc(st_g[t], 16)

                def body(it):
                    last = isinstance(it, int)
                    for u in range(2):
                        unit = it * 2 + u
                        if not last:
                            load_operands(unit + 2, q_mx[u], k_mx[u], ld_mx[u])
                        if not (last and u == 1):
                            sp.wait_ge(s_st, unit * NS + 1)
                            load_operands(unit + 1, q_st[1 - u], k_st[1 - u], ld_st[1 - u])
                            store_rows(unit + 1, 1 - u)
                        if not last and u == 0:
                            sp.wait_ge(s_f1, it * HT + HT)
                            sp.dma_start(xf[:], xf_dram[bass.ds(it + 1, 1)].rearrange("a p t k n -> (a p) t k n")).then_inc(ld_xf, 16)
                    store_gates(it)
                pairs(sp, body)
                for t in range(2):
                    sp.wait_ge(st_g[t], 16 + 16 * PAIRS)

            @block.tensor
            def _(pe):
                pe.sem_inc(s_st, 1)
                pe.sem_inc(s_av, AV_CREDIT)
                pe.sem_inc(s_f2, 1)

                def scores(it, n):
                    unit, u, nth_pair, s = place(it, n)
                    g, parts, _ = STEPS[s]
                    if s == 0:
                        pe.wait_ge(ld_st[u], nth_pair * 64 + 64)
                        pe.wait_ge(ld_mr[u], nth_pair * 32 + 32)
                    if not before(it, n, 2):
                        pe.wait_ge(s_exp, unit * NS + (s - 1))
                    for key, q0, at in parts:
                        out = st_ps[:, n % 2, at:at + G - q0]
                        kt = k_st[u][0:98, key * P:(key + 1) * P]
                        diagonal = key >= JT * g
                        last = nc.tensor.matmul(out, kt, q_st[u][0:98, g * G + q0:(g + 1) * G], start=True, stop=not diagonal)
                        if diagonal:
                            last = nc.tensor.matmul(out[:, 0:P], kept["identb"][:], kept["mask_kq"][:], start=False, stop=True)
                    last.then_inc(s_st, 1)

                def maxima(unit, u, nth_pair, r):
                    if r == 0:
                        pe.wait_ge(ld_mx[u], nth_pair * 64 + 64)
                    pe.wait_ge(s_mr, unit * NR + r)
                    if r == 2:
                        pe.wait_ge(s_row, unit)
                    round_scores(nc, mx_ps[:, r % 2], q_mx[u], k_mx[u], kept, r).then_inc(s_mx, 1)

                def transpose_maxima(unit, follows):
                    pe.wait_ge(s_mh, unit + 1)
                    pe.wait_ge(s_mr, unit * NR + (NR + follows))
                    nc.tensor.transpose(mx_ps[0:2 * QB, 0, 0:P // 2].bitcast(F16), m_ht[:].rearrange("p t i -> p (t i)"),
                                        kept["ident16"][:]).then_inc(s_tm, 1)

                def weighted(it, n):
                    unit, u, _, s = place(it, n)
                    g, parts, _ = STEPS[s]
                    if s == 0:
                        pe.wait_ge(s_vs, unit + 1)
                    if parts[0][0] == 0:
                        pe.wait_ge(s_avc, unit * NG + (g + 1))
                    split_done(pe, unit * NS + (s + 1))
                    for key, q0, at in parts:
                        for w, slot, v0 in ((w_hd, n % HD_RING, 0), (w_tl, n % TL_RING, DH)):
                            for i in range(q0 // P, JT):
                                c = at + i * P - q0
                                last = nc.tensor.matmul(av[:, i, v0:VW], w[:, slot, c:c + P], v_st[:, u, key, v0:VW],
                                                        start=(key == 0 and w is w_hd and i == 0),
                                                        stop=(key == JT * g + JT - 1 and w is w_tl and i == JT - 1),
                                                        skip_group_check=True)
                    last.then_inc(s_av, 1)

                def hidden(it, m, h):
                    if h == 0:
                        if m == 0:
                            pe.wait_ge(ld_xf, it * 16 + 16)
                            pe.wait_ge(s_ga, it * 2 + 1)
                        else:
                            pe.wait_ge(s_re, it * HT + m)
                    for k in (2 * h, 2 * h + 1):
                        for t in range(2):
                            last = nc.tensor.matmul(ff_ps[:, 0:FT], kept["fc_T"][:, k, m * P:(m + 1) * P], xf[:, t, k],
                                                    start=(k == 0 and t == 0), stop=(k == KT - 1 and t == 1))
                    if h == 1:
                        last.then_inc(s_f1, 1)

                def outward(it, t, c, h):
                    if h == 0:
                        if t == 0:
                            if c == 0:
                                pe.wait_ge(s_re, it * HT + HT)
                            pe.wait_ge(s_sl, it * HT + (2 * c + 4))
                        elif c == 0:
                            pe.wait_ge(s_ga, it * 2 + 2)
                    m = 2 * c + h
                    for w in (s_hd, s_tl):
                        last = nc.tensor.matmul(ff_ps[:], w[:, m, t * P:(t + 1) * P], kept["proj_T"][:, m],
                                                start=(m == 0 and w is s_hd), stop=(m == HT - 1 and w is s_tl))
                    if c == 4 and h == 1:
                        last.then_inc(s_f2, 1)

                pe.sem_inc(s_mx, NR)
                transpose_maxima(0, 0)
                pe.wait_ge(s_row, 1)
                maxima(1, 1, 0, 0)
                maxima(1, 1, 0, 1)
                pe.wait_ge(s_set, 2)
                for n in range(1, MX_LEAD - NS):
                    maxima(1, 1, 0, 2 * n)
                    maxima(1, 1, 0, 2 * n + 1)
                    if n <= LAG:
                        scores(0, n - 1)

                def step(it, n):
                    pair, m = it + n // N2, n % N2
                    def feed_forward(h):
                        if m in F1_AT:
                            hidden(pair, F1_AT[m], h)
                        if m in F2_AT:
                            outward(pair, *F2_AT[m], h)

                    ahead = exists(it, n + MX_LEAD)
                    unit, u, nth_pair, s = place(it, n + MX_LEAD)
                    feed_forward(0)
                    if exists(it, n + LAG):
                        scores(it, n + LAG)
                    if ahead:
                        maxima(unit, u, nth_pair, 2 * s)
                    feed_forward(1)
                    weighted(it, n)
                    if ahead:
                        maxima(unit, u, nth_pair, 2 * s + 1)
                    if s == 0 and exists(it, n + MX_LEAD - 1):
                        transpose_maxima(unit - 1, 2 if ahead else 0)
                all_steps(pe, step)

            @block.scalar
            def _(act):
                act.sem_inc(s_avc, 1)

                def weights(it, n, between=None):
                    unit, u, _, s = place(it, n)
                    cols = STEPS[s][2]
                    scores = st_ps[:, n % 2, 0:cols]
                    act.wait_ge(s_st, unit * NS + (s + 2))
                    if not before(it, n, HD_RING):
                        act.wait_ge(s_av, unit * NS + (s + AV_CREDIT + 1 - HD_RING))
                    nc.scalar.activation(w_hd[:, n % HD_RING, 0:cols], scores, ACT.Exp, scale=SCALE).then_inc(s_head, 1)
                    if between:
                        between()
                    if not before(it, n, W_RING):
                        split_done(act, unit * NS + (s + 1 - W_RING))
                    nc.scalar.activation(w32[:, n % W_RING, 0:cols], scores, ACT.Exp, scale=SCALE).then_inc(s_exp, 1)

                def copy_out(it, n):
                    unit, u, _, s = place(it, n)
                    g = STEPS[s][0]
                    act.wait_ge(s_av, unit * NS + (s + AV_CREDIT + 1))
                    if g == 0:
                        act.wait_ge(s_ot, unit + 1)
                    nc.scalar.activation(o_raw[:, u, JT * g:JT * (g + 1)], av, ACT.Copy).then_inc(s_avc, 1)

                def relu(it, m):
                    act.wait_ge(s_f1, it * HT + (m + 1))
                    act.wait_ge(s_sl, it * HT + (m + 1))
                    nc.scalar.activation(r32[:, m % 2], ff_ps[:, 0:FT], ACT.Relu, scale=0.25).then_inc(s_re, 1)

                def gate_tanh(it, t):
                    act.wait_ge(s_f2, it * 2 + (t + 2))
                    act.wait_ge(st_g[t], it * 16 + 16)
                    nc.scalar.activation(g32[:, t], ff_ps[:], ACT.Tanh, scale=kept["ffn_scale"][:]).then_inc(s_e, 1)

                for n in range(LAG):
                    weights(0, n)

                def step(it, n):
                    pair, m, s = it + n // N2, n % N2, n % NS
                    if m - 1 in F1_AT:
                        relu(pair, F1_AT[m - 1])
                    if m - 1 in F2_AT and F2_AT[m - 1][1] == 4:
                        gate_tanh(pair, F2_AT[m - 1][0])
                    ends = s == NS - 1 or STEPS[s + 1][0] != STEPS[s][0]
                    if exists(it, n + LAG):
                        weights(it, n + LAG, (lambda: copy_out(it, n)) if ends else None)
                    elif ends:
                        copy_out(it, n)
                all_steps(act, step)

            @block.gpsimd
            def _(pool):
                pool.sem_inc(s_sl, 2)

                def tail(it, n):
                    unit, u, _, s = place(it, n)
                    c = slice(0, POOL_COLS[u][s])
                    pool.wait_ge(s_exp, unit * NS + (s + 1))
                    pool.wait_ge(s_head, unit * NS + (s + 1))
                    if not before(it, n, TL_RING):
                        pool.wait_ge(s_av, unit * NS + (s + AV_CREDIT + 1 - TL_RING))
                    nc.gpsimd.tensor_tensor(w_tl[:, n % TL_RING, c], w32[:, n % W_RING, c], w_hd[:, n % HD_RING, c],
                                            ALU.subtract).then_inc(s_tlp, 1)

                def square(it, m):
                    pool.wait_ge(s_re, it * HT + (m + 1))
                    if m == 0:
                        pool.wait_ge(s_f2, it * 2 + 1)
                    nc.gpsimd.tensor_tensor(r32[:, m % 2], r32[:, m % 2], r32[:, m % 2], ALU.mult).then_inc(s_sq, 1)
                    pool.wait_ge(s_sq, it * HT + (m + 1))
                    bare(pool, s_bare)
                    nc.gpsimd.tensor_scalar(s_hd[:, m], r32[:, m % 2], 1.0, 0.0, ALU.mult, ALU.add).then_inc(s_sh, 1)
                    pool.wait_ge(s_sh, it * HT + (m + 1))
                    nc.gpsimd.tensor_tensor(s_tl[:, m], r32[:, m % 2], s_hd[:, m], ALU.subtract).then_inc(s_sl, 1)

                def normalise(unit, u):
                    pool.wait_ge(s_rd, unit + 1)
                    o = o_raw[:, u, :, 0:DH]
                    nc.gpsimd.tensor_tensor(o, o, o_raw[:, u, :, DH:2 * DH], ALU.add).then_inc(s_os, 1)
                    pool.wait_ge(s_os, unit + 1)
                    nc.gpsimd.tensor_tensor(o, o, rden[:].rearrange("p (i a) -> p i a", a=1).to_broadcast([P, QB, DH]),
                                            ALU.mult).then_inc(s_on, 1)

                for n in range(TAIL_LAG):
                    tail(0, n)

                def step(it, n):
                    pair, m, s = it + n // N2, n % N2, n % NS
                    if exists(it, n + TAIL_LAG):
                        tail(it, n + TAIL_LAG)
                    if m - 1 in F1_AT:
                        square(pair, F1_AT[m - 1])
                    if s == 2 and not before(it, n, NS):
                        unit, u, _, _ = place(it, n)
                        normalise(unit - 1, 1 - u)
                all_steps(pool, step)
                normalise(UNITS - 1, 1)

            @block.vector
            def _(dve):
                dve.sem_inc(s_mr, NR + 1)
                dve.sem_inc(s_ot, 2)
                dve.sem_inc(s_ga, 1)
                for k in k_st:
                    nc.vector.memset(k[96:98, :], 256.0).then_inc(s_set, 1)
                dve.wait_ge(s_set, 2)

                def reduce(unit, r):
                    dve.wait_ge(s_mx, unit * NR + (r + 1))
                    round_maximum(nc, mx_ps[:, r % 2], mx, r).then_inc(s_mr, 1)

                def split_maxima(unit):
                    dve.wait_ge(s_mr, unit * NR + (NR + 1))
                    nc.vector.tensor_reduce(mm[:], mx[:].rearrange("p c i -> p i c"), AX.X, ALU.max).then_inc(s_m, 1)
                    dve.wait_ge(s_m, unit * 3 + 1)
                    nc.vector.tensor_scalar(mneg[:], mm[:], -1.0 / 256, float(P_SHIFT * np.log(2.0) / SCALE / 256),
                                            ALU.mult, ALU.add).then_inc(s_m, 1)
                    dve.wait_ge(s_m, unit * 3 + 2)
                    nc.vector.tensor_copy(m_ht[:, 0], mneg[:]).then_inc(s_m, 1)
                    dve.wait_ge(s_m, unit * 3 + 3)
                    nc.vector.tensor_tensor(m_ht[:, 1], mneg[:], m_ht[:, 0], ALU.subtract).then_inc(s_mh, 1)

                def copy_rows(unit, u, nth_pair):
                    dve.wait_ge(s_tm, unit + 1)
                    if not (isinstance(unit, int) and unit == 0):
                        v, p = (1 - u), (nth_pair if u == 1 else nth_pair - 1)
                        dve.wait_ge(ld_mr[v], p * 32 + 32)
                    nc.vector.tensor_copy(m_rows[:], mx_ps[0:2 * QB, 0, 0:P // 2].bitcast(F16)).then_inc(s_row, 1)

                def place_v(unit, u):
                    bare(dve, s_bare)
                    nc.vector.tensor_copy(v_st[:, u], v_all[:, bass.ds(unit, 1)].rearrange("p a i v -> p (a i) v")).then_inc(s_vs, 1)

                def tail(it, n):
                    unit, u, _, s = place(it, n)
                    c = slice(POOL_COLS[u][s], STEPS[s][2])
                    dve.wait_ge(s_exp, unit * NS + (s + 1))
                    dve.wait_ge(s_head, unit * NS + (s + 1))
                    if not before(it, n, TL_RING):
                        dve.wait_ge(s_av, unit * NS + (s + AV_CREDIT + 1 - TL_RING))
                    nc.vector.tensor_tensor(w_tl[:, n % TL_RING, c], w32[:, n % W_RING, c], w_hd[:, n % HD_RING, c],
                                            ALU.subtract).then_inc(s_tld, 1)

                def reciprocals(unit, u):
                    dve.wait_ge(s_avc, unit * NG + (NG + 1))
                    nc.vector.reciprocal(rden[:], o_raw[:, u, :, 2 * DH]).then_inc(s_rd, 1)

                def split_output(unit, u):
                    dve.wait_ge(s_on, unit + 1)
                    at = v_all[:, bass.ds(unit, 1)].rearrange("p a i v -> p (a i) v")
                    o = o_raw[:, u, :, 0:DH]
                    bare(dve, s_bare)
                    nc.vector.tensor_copy(at[:, :, 0:DH], o).then_inc(s_oh, 1)
                    dve.wait_ge(s_oh, unit + 1)
                    nc.vector.tensor_tensor(at[:, :, DH:2 * DH], o, at[:, :, 0:DH], ALU.subtract).then_inc(s_ot, 1)

                def gate(it, t):
                    dve.wait_ge(s_e, it * 2 + (t + 1))
                    nc.vector.scalar_tensor_tensor(g32[:, t], g32[:, t], 1.0, ff_ps[:], ALU.add, ALU.mult).then_inc(s_ga, 1)

                split_maxima(0)
                copy_rows(0, 0, 0)
                reduce(1, 0)
                reduce(1, 1)
                place_v(0, 0)
                for n in range(1, MX_LEAD - NS):
                    reduce(1, 2 * n)
                    reduce(1, 2 * n + 1)
                    if n <= TAIL_LAG:
                        tail(0, n - 1)

                def step(it, n):
                    pair, m, s = it + n // N2, n % N2, n % NS
                    unit, u, _, _ = place(it, n)
                    ahead = exists(it, n + MX_LEAD)
                    mx_unit, _, _, mx_s = place(it, n + MX_LEAD)
                    if ahead:
                        reduce(mx_unit, 2 * mx_s)
                    if exists(it, n + TAIL_LAG):
                        tail(it, n + TAIL_LAG)
                    if ahead:
                        reduce(mx_unit, 2 * mx_s + 1)
                        if mx_s == NS - 1:
                            split_maxima(mx_unit)
                    if mx_s == 0 and exists(it, n + MX_LEAD - 1):
                        copy_rows(*place(it, n + MX_LEAD - 1)[:3])
                    if s == 10 and exists(it, n + NS):
                        dve.wait_ge(s_av, unit * NS + AV_CREDIT)
                        place_v(unit + 1, 1 - u)
                    if m - 1 in F2_AT and F2_AT[m - 1][1] == 4:
                        gate(pair, F2_AT[m - 1][0])
                    if not before(it, n, NS):
                        if s == 1:
                            reciprocals(unit - 1, 1 - u)
                        if s == 4:
                            split_output(unit - 1, 1 - u)
                all_steps(dve, step)
                reciprocals(UNITS - 1, 1)
                split_output(UNITS - 1, 1)


def finish_block(nc, x, out, gate_dram, kept):
    RX = 4
    with ExitStack() as ctx:
        def sb(name, shape, dt):
            return ctx.enter_context(nc.sbuf_tensor(name, shape, dt))

        def sem(name):
            return ctx.enter_context(nc.semaphore(name))

        xt = sb("xt", [P, RX, D], F32)
        gt = sb("gt", [P, RX, D], F32)
        og = sb("og", [P, 2, 2, D], F16)
        oT = sb("oT", [P, 2, 2, KT, P], F16)
        y1 = sb("y1", [P, 2, D], F32)
        y2 = sb("y2", [P, 2, D], F32)
        y3 = sb("y3", [P, RX, D], F32)
        tps = ctx.enter_context(nc.psum_tensor("o_tp", [P, 2, 2, D], F16))
        pso = ctx.enter_context(nc.psum_tensor("o_pj", [P, 2, D], F32))
        v_all = kept["v_all"]

        ld = [sem(f"ld_t{r}") for r in range(RX)]
        st = [sem(f"st_t{r}") for r in range(RX)]
        s_bare = sem("s_bare_f")
        s_g = sem("s_og")
        s_t, s_c = sem("s_ot_t"), sem("s_ot_c")
        s_p = sem("s_op")
        s_y1 = sem("s_y1")
        s_y2 = sem("s_y2")
        s_y3 = sem("s_y3")
        TURNS = QB // 2

        def turns(eng, body):
            with eng.Fori(0, TURNS - 1) as j:
                for r in range(RX):
                    body(j, r, True)
            for r in range(RX):
                body(TURNS - 1, r, r < 2)

        with nc.Block() as block:
            @block.sync
            def _(sp):
                for r in range(RX):
                    sp.sem_inc(st[r], 16)

                def load(j, r):
                    sp.dma_start(xt[:, r], x[r % 2, bass.ds(j * (2 * P) + r // 2 * P, P), :]).then_inc(ld[r], 16)
                    sp.dma_start(gt[:, r], gate_dram[bass.ds(j * 2 + (QB * (r % 2) + r // 2), 1)]
                                 .rearrange("a p d -> (a p) d")).then_inc(ld[r], 16)

                for r in range(RX):
                    load(0, r)

                def body(j, r, ahead):
                    sp.wait_ge(s_y3, j * RX + (r + 3))
                    sp.dma_start(out[r % 2, bass.ds(j * (2 * P) + r // 2 * P, P), :], y3[:, r]).then_inc(st[r], 16)
                    if not isinstance(j, int):
                        load(j + 1, r)
                turns(sp, body)
                for r in range(RX):
                    sp.wait_ge(st[r], 16 + 16 * TURNS)

            @block.tensor
            def _(pe):
                pe.sem_inc(s_p, 2)
                pe.sem_inc(s_t, 2)

                def transpose(n, t):
                    pe.wait_ge(s_g, n + 1)
                    pe.wait_ge(s_c, n + 1)
                    for part in range(2):
                        for k in range(KT):
                            last = nc.tensor.transpose(tps[:, t, part, k * P:(k + 1) * P], og[:, t, part, k * P:(k + 1) * P],
                                                       kept["ident16"][:])
                    last.then_inc(s_t, 1)

                for n in range(2):
                    transpose(n, n)

                def body(j, r, ahead):
                    n, t = j * RX + r, r % 2
                    pe.wait_ge(s_c, n + 3)
                    pe.wait_ge(s_y1, n + 1)
                    for k in range(KT):
                        for i, (a, b) in enumerate(((0, "wo_head"), (0, "wo_tail"), (1, "wo_head"))):
                            last = nc.tensor.matmul(pso[:, t], oT[:, t, a, k], kept[b][:, k],
                                                    start=(k == 0 and i == 0), stop=(k == KT - 1 and i == 2))
                    last.then_inc(s_p, 1)
                    if ahead:
                        transpose(n + 2, t)
                turns(pe, body)

            @block.scalar
            def _(act):
                act.sem_inc(s_c, 2)

                def copy(n, t):
                    act.wait_ge(s_t, n + 3)
                    act.wait_ge(s_p, n + 1)
                    nc.scalar.activation(oT[:, t].rearrange("p a k n -> p (a k n)"), tps[:, t].rearrange("p a n -> p (a n)"),
                                         ACT.Copy).then_inc(s_c, 1)

                for n in range(2):
                    copy(n, n)

                def body(j, r, ahead):
                    n = j * RX + r
                    if ahead:
                        copy(n + 2, r % 2)
                turns(act, body)

            @block.gpsimd
            def _(pool):
                pool.sem_inc(s_y2, 2)
                with pool.Fori(0, TURNS) as j:
                    for r in range(RX):
                        n = j * RX + r
                        pool.wait_ge(s_y1, n + 3)
                        pool.wait_ge(s_y3, n + 1)
                        pool.wait_ge(ld[r], j * 32 + 32)
                        nc.gpsimd.tensor_tensor(y2[:, r % 2], y1[:, r % 2], gt[:, r], ALU.mult).then_inc(s_y2, 1)

            @block.vector
            def _(dve):
                dve.sem_inc(s_y1, 2)
                dve.sem_inc(s_y3, 2)

                def gather(j, r):
                    n, t = j * RX + r, r % 2
                    dve.wait_ge(s_t, n + 1)
                    bare(dve, s_bare)
                    for part in range(2):
                        heads = v_all[:, H * t:H * (t + 1), bass.ds(j * 2 + r // 2, 1), DH * part:DH * (part + 1)]
                        last = nc.vector.tensor_copy(og[:, t, part].rearrange("p (h d) -> p h d", h=H),
                                                     heads.rearrange("p h a d -> p (h a) d"))
                    last.then_inc(s_g, 1)

                def residual(j, r):
                    dve.wait_ge(s_y2, j * RX + (r + 3))
                    dve.wait_ge(ld[r], j * 32 + 32)
                    dve.wait_ge(st[r], j * 16 + 16)
                    nc.vector.scalar_tensor_tensor(y3[:, r], y2[:, r % 2], kept["ffn_scale"][:], xt[:, r],
                                                   ALU.mult, ALU.add).then_inc(s_y3, 1)

                gather(0, 0)
                gather(0, 1)

                def body(j, r, ahead):
                    if ahead:
                        gather(j + (r + 2) // RX, (r + 2) % RX)
                    n, t = j * RX + r, r % 2
                    dve.wait_ge(s_p, n + 3)
                    dve.wait_ge(s_y2, n + 1)
                    nc.vector.scalar_tensor_tensor(y1[:, t], pso[:, t], kept["out_scale"][:], kept["out_bias"][:],
                                                   ALU.mult, ALU.add).then_inc(s_y1, 1)
                    if r > 0:
                        residual(j, r - 1)
                    if r == RX - 1:
                        residual(j, r)
                turns(dve, body)


def build(nc, X, ln_g, ln_b, Wq, bq, Wk, bk, Wv, bv, Wo, bo, w_fc, w_proj, out):
    with ExitStack() as ctx:
        def sb(name, shape, dt):
            return ctx.enter_context(nc.sbuf_tensor(name, shape, dt))
        kept = dict(
            ident32=sb("ident32", [P, P], F32), ident16=sb("ident16", [P, P], F16), identb=sb("identb", [P, P], BF16),
            mask_kq=sb("mask_kq", [P, P], BF16), mask_qk=sb("mask_qk", [P, P], BF16),
            half=sb("half", [P, JT], F32),
            scale=sb("scale", [P, 4], F32), unscale=sb("unscale", [P, 4], F32),
            amean=sb("amean", [P, 2], F32), ffn_scale=sb("ffn_scale", [P, 1], F32), out_scale=sb("out_scale", [P, 1], F32),
            qk_bias=sb("qk_bias", [P, 2, KT], F32), out_bias=sb("out_bias", [P, D], F32),
            wo_head=sb("wo_head", [P, KT, D], F16), wo_tail=sb("wo_tail", [P, KT, D], F16),
            fc_T=sb("fc_T", [P, KT, HID], F16), proj_T=sb("proj_T", [P, HT, D], F16),
        )
        qk_dram = nc.dram_tensor("qk_split", (UNITS, 2, 2, DH, S), F16, kind="Internal").ap()
        xf_dram = nc.dram_tensor("xf_split", (NT // 2, P, 2, KT, 2 * P), F16, kind="Internal").ap()
        with ExitStack() as c2:
            kept["w_head"] = c2.enter_context(nc.sbuf_tensor("w_head", [P, 3, KT, D], F16))
            kept["w_tail"] = c2.enter_context(nc.sbuf_tensor("w_tail", [P, 3, KT, D], F16))
            kept["xin"] = c2.enter_context(nc.sbuf_tensor("xin", [P, 2, JT, D], F32))
            weights_block(nc, X, (ln_g, ln_b, Wq, bq, Wk, bk, Wv, bv, Wo, bo, w_fc, w_proj), kept)
            kept["v_all"] = ctx.enter_context(nc.sbuf_tensor("v_all", [P, UNITS, S // P, VW], F16, side="right"))
            kept["mx"] = ctx.enter_context(nc.sbuf_tensor("mx", [P, NG, QB], F32, side="right"))
            project_block(nc, X, qk_dram, xf_dram, kept)
        gate_dram = nc.dram_tensor("gate", (NT, P, D), F32, kind="Internal").ap()
        attend_block(nc, qk_dram, xf_dram, gate_dram, kept)
        finish_block(nc, X, out, gate_dram, kept)


_INS = ["L0_attn_X", "L0_attn_ln_g", "L0_attn_ln_b", "L0_attn_Wq", "L0_attn_bq", "L0_attn_Wk", "L0_attn_bk", "L0_attn_Wv",
        "L0_attn_bv", "L0_attn_Wo", "L0_attn_bo", "L0_ffn_w_fc", "L0_ffn_w_proj"]


def kernel(**inputs):
    import concourse.bacc as _bacc
    from concourse.bass_utils import run_bass_kernel_spmd as _run

    nc = _bacc.Bacc("TRN2", target_bir_lowering=False, num_devices=1)
    arrays, args = {}, []
    for name in _INS:
        a = np.ascontiguousarray(inputs[name])
        arrays[f"in_{name}"] = a
        args.append(nc.dram_tensor(f"in_{name}", a.shape, mybir.dt.from_np(a.dtype), kind="ExternalInput").ap())
    out = nc.dram_tensor("out_0", (B, S, D), F32, kind="ExternalOutput").ap()
    build(nc, *args, out)
    r = _run(nc, [arrays], core_ids=[0])
    return r.results[0]["out_0"]
```
